# Optimizing a Trainium2 kernel written in Bass

```python
import numpy as np
import jax
import jax.numpy as jnp

def _softmax(x, axis=-1):
    return jax.nn.softmax(x, axis=axis)

def _gelu(x):
    return jax.nn.gelu(x, approximate=True)

def _silu(x):
    return jax.nn.silu(x)

def _sigmoid(x):
    return jax.nn.sigmoid(x)

def _layernorm(x, axis=-1, eps=1e-05):
    m = jnp.mean(x, axis=axis, keepdims=True)
    v = jnp.var(x, axis=axis, keepdims=True)
    return (x - m) / jnp.sqrt(v + eps)

def _scatter_add(tgt, idx, src, axis=0):
    return tgt.at[idx].add(src)

def _segment_sum(src, seg, n):
    return jax.ops.segment_sum(src, seg, n)
kernel_name = 'mk_hybrid_d1_jaxref_r8_1d3fa1'

def setup_inputs(seed: int=0):
    np.random.seed(seed)
    _w = jnp.asarray

    def _L0_attn_a_setup():
        import jax, jax.numpy as jnp
        import numpy as np
        import math
        B, T, H = (2, 256, 256)
        NH = 16
        HS = H // NH
        ROPE_BASE = 10000.0

        def apply_rope(x):
            hs = x.shape[-1]
            t = jnp.arange(x.shape[2], dtype=jnp.float32)
            inv_freq = 1.0 / ROPE_BASE ** (jnp.arange(0, hs, 2, dtype=jnp.float32) / hs)
            ang = t[:, None] * inv_freq[None, :]
            cos, sin = (jnp.cos(ang), jnp.sin(ang))
            x1, x2 = (x[..., 0::2], x[..., 1::2])
            out_even = x1 * cos - x2 * sin
            out_odd = x1 * sin + x2 * cos
            return jnp.stack([out_even, out_odd], axis=-1).reshape(x.shape)
        key = jax.random.key(seed)
        ks = jax.random.split(key, 9)
        s = 1.0 / math.sqrt(H)
        inp = {'x': jax.random.normal(ks[0], (B, T, H), dtype=jnp.float32)}
        for i, name in enumerate(['q', 'k', 'v', 'o']):
            inp[f'W{name}'] = jax.random.normal(ks[1 + i], (H, H), dtype=jnp.float32) * s
            inp[f'b{name}'] = jax.random.normal(ks[5 + i], (H,), dtype=jnp.float32) * 0.01
        return inp
    _L0_attn_a_in = _L0_attn_a_setup()

    def _L0_attn_b_setup():
        import jax, jax.numpy as jnp
        import numpy as np
        from jax import lax
        B, S, HID = (4, 256, 256)
        NH, DK, DV = (32, 64, 64)
        KDIM, VDIM = (NH * DK, NH * DV)
        CONV_DIM = 2 * KDIM + VDIM
        K_CONV = 4
        EPS = 1e-06

        def _l2norm(x):
            return x * lax.rsqrt(jnp.sum(x * x, -1, keepdims=True) + EPS)
        key = jax.random.key(seed)
        ks = jax.random.split(key, 8)
        return {'hidden_states': jax.random.normal(ks[0], (B, S, HID), jnp.float32), 'w_qkvz': jax.random.normal(ks[1], (2 * KDIM + 2 * VDIM, HID), jnp.float32) * 0.02, 'w_ba': jax.random.normal(ks[2], (2 * NH, HID), jnp.float32) * 0.02, 'conv_w': jax.random.normal(ks[3], (CONV_DIM, 1, K_CONV), jnp.float32) * 0.5, 'A_log': jnp.log(jax.random.uniform(ks[4], (NH,), jnp.float32, 0.1, 16.0)), 'dt_bias': jnp.ones((NH,), jnp.float32), 'norm_weight': jnp.ones((DV,), jnp.float32), 'w_out': jax.random.normal(ks[5], (HID, VDIM), jnp.float32) * 0.02}
    _L0_attn_b_in = _L0_attn_b_setup()

    def _L0_ffn_setup():
        import jax, jax.numpy as jnp
        import numpy as np
        H = 256
        I = 176
        E = 16
        K = 2
        N_SHARED = 2
        IS = I * N_SHARED
        ROUTED_SCALE = 1.0
        CAPACITY = 128

        def _moe_forward(hidden_states, gate_w, w_gate, w_up, w_down, ws_gate, ws_up, ws_down):
            B, S, _ = hidden_states.shape
            x = hidden_states.reshape(-1, H)
            T = x.shape[0]
            logits = jnp.einsum('th,eh->te', x.astype(jnp.float32), gate_w.astype(jnp.float32))
            scores = jax.nn.softmax(logits, axis=-1)
            topk_w, topk_idx = jax.lax.top_k(scores, K)
            topk_w = (topk_w * ROUTED_SCALE).astype(x.dtype)
            flat_idx = topk_idx.reshape(-1)
            order = jnp.argsort(flat_idx)
            sorted_e = flat_idx[order]
            sorted_t = order // K
            counts = jnp.bincount(flat_idx, length=E)
            starts = jnp.cumsum(counts) - counts
            pos = jnp.arange(T * K) - starts[sorted_e]
            buf = jnp.zeros((E, CAPACITY, H), x.dtype).at[sorted_e, pos].set(x[sorted_t], mode='drop')
            g = jax.nn.silu(jnp.einsum('ech,ehi->eci', buf, w_gate))
            u = jnp.einsum('ech,ehi->eci', buf, w_up)
            expert_out = jnp.einsum('eci,eih->ech', g * u, w_down)
            gathered = expert_out[sorted_e, pos]
            out_flat = jnp.zeros((T * K, H), x.dtype).at[order].set(gathered)
            y = (out_flat.reshape(T, K, H) * topk_w[..., None]).sum(axis=1)
            sh = jnp.einsum('ti,ih->th', jax.nn.silu(x @ ws_gate) * (x @ ws_up), ws_down)
            return (y + sh).reshape(B, S, H)
        key = jax.random.key(seed)
        ks = jax.random.split(key, 8)
        B, S = (2, 128)
        scale = 0.02
        return {'hidden_states': jax.random.normal(ks[0], (B, S, H), jnp.float32), 'gate_w': jax.random.normal(ks[1], (E, H), jnp.float32) * scale, 'w_gate': jax.random.normal(ks[2], (E, H, I), jnp.float32) * scale, 'w_up': jax.random.normal(ks[3], (E, H, I), jnp.float32) * scale, 'w_down': jax.random.normal(ks[4], (E, I, H), jnp.float32) * scale, 'ws_gate': jax.random.normal(ks[5], (H, IS), jnp.float32) * scale, 'ws_up': jax.random.normal(ks[6], (H, IS), jnp.float32) * scale, 'ws_down': jax.random.normal(ks[7], (IS, H), jnp.float32) * scale}
    _L0_ffn_in = _L0_ffn_setup()
    _d = {'L0_attn_a_x': _L0_attn_a_in['x'], 'L0_attn_a_Wq': _L0_attn_a_in['Wq'], 'L0_attn_a_bq': _L0_attn_a_in['bq'], 'L0_attn_a_Wk': _L0_attn_a_in['Wk'], 'L0_attn_a_bk': _L0_attn_a_in['bk'], 'L0_attn_a_Wv': _L0_attn_a_in['Wv'], 'L0_attn_a_bv': _L0_attn_a_in['bv'], 'L0_attn_a_Wo': _L0_attn_a_in['Wo'], 'L0_attn_a_bo': _L0_attn_a_in['bo'], 'L0_attn_b_w_qkvz': _L0_attn_b_in['w_qkvz'], 'L0_attn_b_w_ba': _L0_attn_b_in['w_ba'], 'L0_attn_b_conv_w': _L0_attn_b_in['conv_w'], 'L0_attn_b_A_log': _L0_attn_b_in['A_log'], 'L0_attn_b_dt_bias': _L0_attn_b_in['dt_bias'], 'L0_attn_b_norm_weight': _L0_attn_b_in['norm_weight'], 'L0_attn_b_w_out': _L0_attn_b_in['w_out'], 'L0_ffn_gate_w': _L0_ffn_in['gate_w'], 'L0_ffn_w_gate': _L0_ffn_in['w_gate'], 'L0_ffn_w_up': _L0_ffn_in['w_up'], 'L0_ffn_w_down': _L0_ffn_in['w_down'], 'L0_ffn_ws_gate': _L0_ffn_in['ws_gate'], 'L0_ffn_ws_up': _L0_ffn_in['ws_up'], 'L0_ffn_ws_down': _L0_ffn_in['ws_down']}
    _x0 = _d['L0_attn_a_x']
    _d['L0_attn_a_x'] = jax.random.normal(jax.random.fold_in(jax.random.key(seed), 1), (4, 256, 256), dtype=_x0.dtype)
    del _x0
    return _d

def reference(L0_attn_a_x, L0_attn_a_Wq, L0_attn_a_bq, L0_attn_a_Wk, L0_attn_a_bk, L0_attn_a_Wv, L0_attn_a_bv, L0_attn_a_Wo, L0_attn_a_bo, L0_attn_b_w_qkvz, L0_attn_b_w_ba, L0_attn_b_conv_w, L0_attn_b_A_log, L0_attn_b_dt_bias, L0_attn_b_norm_weight, L0_attn_b_w_out, L0_ffn_gate_w, L0_ffn_w_gate, L0_ffn_w_up, L0_ffn_w_down, L0_ffn_ws_gate, L0_ffn_ws_up, L0_ffn_ws_down):

    def _L0_attn_a_ref(x, Wq, bq, Wk, bk, Wv, bv, Wo, bo):
        import jax, jax.numpy as jnp
        import numpy as np
        import math
        B, T, H = (2, 256, 256)
        NH = 16
        HS = H // NH
        ROPE_BASE = 10000.0

        def apply_rope(x):
            hs = x.shape[-1]
            t = jnp.arange(x.shape[2], dtype=jnp.float32)
            inv_freq = 1.0 / ROPE_BASE ** (jnp.arange(0, hs, 2, dtype=jnp.float32) / hs)
            ang = t[:, None] * inv_freq[None, :]
            cos, sin = (jnp.cos(ang), jnp.sin(ang))
            x1, x2 = (x[..., 0::2], x[..., 1::2])
            out_even = x1 * cos - x2 * sin
            out_odd = x1 * sin + x2 * cos
            return jnp.stack([out_even, out_odd], axis=-1).reshape(x.shape)
        Bsz, Tl, h = x.shape
        q = (x @ Wq + bq).reshape(Bsz, Tl, NH, HS).transpose(0, 2, 1, 3)
        k = (x @ Wk + bk).reshape(Bsz, Tl, NH, HS).transpose(0, 2, 1, 3)
        v = (x @ Wv + bv).reshape(Bsz, Tl, NH, HS).transpose(0, 2, 1, 3)
        q = apply_rope(q)
        k = apply_rope(k)
        scale = 1.0 / math.sqrt(HS)
        attn = jnp.einsum('bhqd,bhkd->bhqk', q, k) * scale
        attn = jax.nn.softmax(attn, axis=-1)
        tril = jnp.tril(jnp.ones((Tl, Tl), dtype=attn.dtype))
        attn = attn * tril[None, None, :, :]
        out = jnp.einsum('bhqk,bhkd->bhqd', attn, v)
        o = out.transpose(0, 2, 1, 3).reshape(Bsz, Tl, h)
        return o @ Wo + bo

    def _L0_attn_b_ref(hidden_states, w_qkvz, w_ba, conv_w, A_log, dt_bias, norm_weight, w_out):
        import jax, jax.numpy as jnp
        import numpy as np
        from jax import lax
        B, S, HID = (4, 256, 256)
        NH, DK, DV = (32, 64, 64)
        KDIM, VDIM = (NH * DK, NH * DV)
        CONV_DIM = 2 * KDIM + VDIM
        K_CONV = 4
        EPS = 1e-06

        def _l2norm(x):
            return x * lax.rsqrt(jnp.sum(x * x, -1, keepdims=True) + EPS)
        Bsz, Sl, _ = hidden_states.shape
        qkvz = (hidden_states @ w_qkvz.T).reshape(Bsz, Sl, NH, 2 * DK + 2 * DV)
        q, k, v, z = jnp.split(qkvz, [DK, 2 * DK, 2 * DK + DV], axis=-1)
        ba = (hidden_states @ w_ba.T).reshape(Bsz, Sl, NH, 2)
        b, a = (ba[..., 0], ba[..., 1])
        mixed = jnp.concatenate([q.reshape(Bsz, Sl, -1), k.reshape(Bsz, Sl, -1), v.reshape(Bsz, Sl, -1)], -1)
        mixed = jnp.swapaxes(mixed, 1, 2)
        mixed = lax.conv_general_dilated(mixed, conv_w, (1,), [(K_CONV - 1, 0)], dimension_numbers=('NCH', 'OIH', 'NCH'), feature_group_count=CONV_DIM)
        mixed = jnp.swapaxes(mixed, 1, 2)
        qf, kf, vf = jnp.split(mixed, [KDIM, 2 * KDIM], axis=-1)
        q = qf.reshape(Bsz, Sl, NH, DK)
        k = kf.reshape(Bsz, Sl, NH, DK)
        v = vf.reshape(Bsz, Sl, NH, DV)
        g = -jnp.exp(A_log) * jax.nn.softplus(a + dt_bias)
        beta = jax.nn.sigmoid(b)
        q = _l2norm(q) * DK ** (-0.5)
        k = _l2norm(k)
        qs = jnp.moveaxis(q, 1, 0)
        ks_ = jnp.moveaxis(k, 1, 0)
        vs = jnp.moveaxis(v, 1, 0)
        gs = jnp.moveaxis(g, 1, 0)
        bs = jnp.moveaxis(beta, 1, 0)

        def step(Sstate, xs):
            q_t, k_t, v_t, g_t, b_t = xs
            Sstate = Sstate * jnp.exp(g_t)[..., None, None]
            kv = jnp.einsum('bhk,bhkv->bhv', k_t, Sstate)
            delta = (v_t - kv) * b_t[..., None]
            Sstate = Sstate + k_t[..., :, None] * delta[..., None, :]
            o_t = jnp.einsum('bhk,bhkv->bhv', q_t, Sstate)
            return (Sstate, o_t)
        S0 = jnp.zeros((Bsz, NH, DK, DV), q.dtype)
        _, o = lax.scan(step, S0, (qs, ks_, vs, gs, bs))
        o = jnp.moveaxis(o, 0, 1)
        var = jnp.mean(o * o, -1, keepdims=True)
        o = o * lax.rsqrt(var + EPS) * norm_weight * jax.nn.sigmoid(z)
        return o.reshape(Bsz, Sl, VDIM) @ w_out.T

    def _L0_ffn_ref(hidden_states, gate_w, w_gate, w_up, w_down, ws_gate, ws_up, ws_down):
        import jax, jax.numpy as jnp
        import numpy as np
        H = 256
        I = 176
        E = 16
        K = 2
        N_SHARED = 2
        IS = I * N_SHARED
        ROUTED_SCALE = 1.0
        CAPACITY = 128

        def _moe_forward(hidden_states, gate_w, w_gate, w_up, w_down, ws_gate, ws_up, ws_down):
            B, S, _ = hidden_states.shape
            x = hidden_states.reshape(-1, H)
            T = x.shape[0]
            logits = jnp.einsum('th,eh->te', x.astype(jnp.float32), gate_w.astype(jnp.float32))
            scores = jax.nn.softmax(logits, axis=-1)
            topk_w, topk_idx = jax.lax.top_k(scores, K)
            topk_w = (topk_w * ROUTED_SCALE).astype(x.dtype)
            flat_idx = topk_idx.reshape(-1)
            order = jnp.argsort(flat_idx)
            sorted_e = flat_idx[order]
            sorted_t = order // K
            counts = jnp.bincount(flat_idx, length=E)
            starts = jnp.cumsum(counts) - counts
            pos = jnp.arange(T * K) - starts[sorted_e]
            buf = jnp.zeros((E, CAPACITY, H), x.dtype).at[sorted_e, pos].set(x[sorted_t], mode='drop')
            g = jax.nn.silu(jnp.einsum('ech,ehi->eci', buf, w_gate))
            u = jnp.einsum('ech,ehi->eci', buf, w_up)
            expert_out = jnp.einsum('eci,eih->ech', g * u, w_down)
            gathered = expert_out[sorted_e, pos]
            out_flat = jnp.zeros((T * K, H), x.dtype).at[order].set(gathered)
            y = (out_flat.reshape(T, K, H) * topk_w[..., None]).sum(axis=1)
            sh = jnp.einsum('ti,ih->th', jax.nn.silu(x @ ws_gate) * (x @ ws_up), ws_down)
            return (y + sh).reshape(B, S, H)
        return _moe_forward(hidden_states, gate_w, w_gate, w_up, w_down, ws_gate, ws_up, ws_down)
    x = L0_attn_a_x
    x = x + _L0_attn_a_ref(_layernorm(x, axis=-1), L0_attn_a_Wq, L0_attn_a_bq, L0_attn_a_Wk, L0_attn_a_bk, L0_attn_a_Wv, L0_attn_a_bv, L0_attn_a_Wo, L0_attn_a_bo)
    x = x + _L0_ffn_ref(_layernorm(x, axis=-1), L0_ffn_gate_w, L0_ffn_w_gate, L0_ffn_w_up, L0_ffn_w_down, L0_ffn_ws_gate, L0_ffn_ws_up, L0_ffn_ws_down)
    x = x + _L0_attn_b_ref(_layernorm(x, axis=-1), L0_attn_b_w_qkvz, L0_attn_b_w_ba, L0_attn_b_conv_w, L0_attn_b_A_log, L0_attn_b_dt_bias, L0_attn_b_norm_weight, L0_attn_b_w_out)
    x = x + _L0_ffn_ref(_layernorm(x, axis=-1), L0_ffn_gate_w, L0_ffn_w_gate, L0_ffn_w_up, L0_ffn_w_down, L0_ffn_ws_gate, L0_ffn_ws_up, L0_ffn_ws_down)
    return x

_drawn_inputs = setup_inputs


def setup_inputs(seed=0):
    import zlib

    import numpy as np

    out = dict(_drawn_inputs(seed))
    spreads = {'L0_attn_b_dt_bias': (1.0, 0.6), 'L0_attn_b_norm_weight': (1.0, 0.2)}
    factors = {'L0_attn_a_bq': 8.0,
     'L0_attn_a_bk': 8.0,
     'L0_attn_a_bv': 7.673,
     'L0_attn_a_bo': 4.838,
     'L0_ffn_gate_w': 8.0,
     'L0_ffn_w_gate': 8.0,
     'L0_ffn_w_up': 8.0,
     'L0_ffn_w_down': 8.0}
    for name, (base, spread) in spreads.items():
        noise = np.random.default_rng([zlib.crc32(name.encode()), seed]).standard_normal(out[name].shape)
        drawn = base * np.exp(spread * noise) if base else spread * noise
        out[name] = jnp.asarray(drawn.astype(out[name].dtype))
    for name, factor in factors.items():
        out[name] = (out[name] * factor).astype(out[name].dtype)
    return out
```

```python
import numpy as np

import concourse.bass as bass
from concourse import mybir
from contextlib import ExitStack, contextmanager

F32 = mybir.dt.float32
BF16 = mybir.dt.bfloat16
U32 = mybir.dt.uint32
ALU = mybir.AluOpType
ACT = mybir.ActivationFunctionType
AX = mybir.AxisListType

P = 128
B, T, H = 4, 256, 256
NT = B * T // P
KC = H // P
LN_EPS = 1e-5

NHA, HSA = 16, 16
HPT = P // HSA
VPITCH = P + HSA

E, I, CAP = 16, 176, 128
IS = 2 * I
IH = I // 2
SHC = [(0, 128), (128, 128), (256, 96)]

NH, D = 32, 64
NP = NH // 2
TAPS = 4
PADT = T + TAPS - 1
GEPS = 1e-6


class Core:
    pass


def bc(ap, axis, n):
    v = ap.unsqueeze(axis)
    return v.to_broadcast([n if a == axis else s for a, s in enumerate(v.shape)])


@contextmanager
def semaphores(nc):
    taken = []

    def take(name):
        taken.append(nc.alloc_semaphore(name=name))
        return taken[-1]

    yield take
    nc.all_engine_barrier()
    nc.clear_and_free_semaphores(taken)
    nc.all_engine_barrier()


def stage_load(k, I_):
    nc = k.nc
    with semaphores(nc) as take, nc.Block() as block:
        loaded = take("common_loaded")

        @block.sync
        def _(sp):
            xs = I_["x"].rearrange("b (h p) d -> p (b h) d", p=P)
            sp.dma_start(k.X[:, :, :], xs).then_inc(loaded, 16)
            for dst, src in ((k.ident, "ident"), (k.tri_incl, "tri_incl"), (k.tri_strict, "tri_strict")):
                sp.dma_start(dst[:, :], I_[src]).then_inc(loaded, 16)
            for bufs in k.bufs:
                sp.dma_start(bufs.rearrange("(p r) d -> p (r d)", p=P), I_["zeros"]).then_inc(loaded, 16)
            sp.wait_ge(loaded, 4 * 16 + 16 * len(k.bufs))

        @block.gpsimd
        def _(pool):
            pool.memset(k.eps[:, :], LN_EPS)


def stage_attention_a(k, I_):
    nc, X, ident, PS = k.nc, k.X, k.ident, k.PS
    NS = NHA
    with semaphores(nc) as take, ExitStack() as ctx:
        def sb(name, shape, dt=F32):
            return ctx.enter_context(nc.sbuf_tensor(name, shape, dt))

        def sem(name):
            return take(name)

        w_qkv = sb("a_w_qkv", [P, KC, 3 * H])
        b_qkv = sb("a_b_qkv", [P, 3 * H])
        w_o = sb("a_w_o", [P, KC, H])
        b_o = sb("a_b_o", [P, H])
        cos = sb("a_cos", [P, 2, 2, HSA])
        sin = sb("a_sin", [P, 2, 2, HSA])
        head_rows = sb("a_head_rows", [P, HPT])
        stats = sb("a_stats", [P, NT, 6])
        mv = sb("a_mv", [P, NT, 2])
        std = sb("a_std", [P, NT])
        rstd = sb("a_rstd", [P, NT])
        xn = sb("a_xn", [P, 2, H])
        xT = sb("a_xT", [P, KC, T])
        qk = sb("a_qk", [P, 2, 2 * H])
        qk_cos = sb("a_qk_cos", [P, 2, 2 * H])
        qk_sin = sb("a_qk_sin", [P, 2, 2 * H])
        qT = sb("a_qT", [P, 2, T])
        kT = sb("a_kT", [P, 2, HPT, T])
        v_pad = sb("a_v_pad", [P, 2, 2, HPT * VPITCH])
        neg_max = sb("a_neg_max", [P, 4, 2])
        row_sum = sb("a_row_sum", [P, 4, 2])
        row_inv = sb("a_row_inv", [P, 4, 2])
        probs = sb("a_probs", [P, 3, 2, T])
        probsT = sb("a_probsT", [P, 2, 2, 2, T])
        oT = sb("a_oT", [P, 2, T])
        y = sb("a_y", [P, 2, H])

        loaded = sem("a_loaded")
        v_zero = sem("a_v_zero")
        stats_done = sem("a_stats_done")
        mv_done = sem("a_mv_done")
        std_done = sem("a_std_done")
        rstd_done = sem("a_rstd_done")
        xn_done = sem("a_xn_done")
        xT_in_psum = sem("a_xT_in_psum")
        xT_done = sem("a_xT_done")
        qkv_in_psum = sem("a_qkv_in_psum")
        qk_done = sem("a_qk_done")
        rope_parts = sem("a_rope_parts")
        rope_done = sem("a_rope_done")
        qkT_in_psum = sem("a_qkT_in_psum")
        qT_done = sem("a_qT_done")
        kT_done = sem("a_kT_done")
        scores_done = sem("a_scores_done")
        max_done = sem("a_max_done")
        exp_done = sem("a_exp_done")
        inv_done = sem("a_inv_done")
        probs_done = sem("a_probs_done")
        probsT_in_psum = sem("a_probsT_in_psum")
        diag_done = sem("a_diag_done")
        full_done = sem("a_full_done")
        av_done = sem("a_av_done")
        oT_done = sem("a_oT_done")
        y_in_psum = sem("a_y_in_psum")
        y_done = sem("a_y_done")
        x_done = sem("a_x_done")

        SC = [PS[:, j, :].rearrange("p (h t) -> p h t", h=2) for j in range(3)]
        TR = [PS[:, 3 + j, :].rearrange("p (h c t) -> p h c t", h=2, c=2) for j in range(2)]
        TA = PS[:, 5, :]
        OT = [PS[:, 6, 0:T], PS[:, 5, 0:T]]
        YB = PS[:, 7, :].rearrange("p (n d) -> p n d", n=2)

        with nc.Block() as block:

            @block.sync
            def _(sp):
                for dst, name in ((w_qkv, "a_w_qkv"), (w_o, "a_w_o"), (cos, "a_cos"), (sin, "a_sin"),
                                  (head_rows, "a_head_rows")):
                    sp.dma_start(dst[tuple(slice(None) for _ in dst.shape)], I_[name]).then_inc(loaded, 16)
                sp.dma_start(b_qkv[:, :], I_["a_b_qkv"].partition_broadcast(P)).then_inc(loaded, 16)
                sp.dma_start(b_o[:, :], I_["a_b_o"].partition_broadcast(P)).then_inc(loaded, 16)
                sp.wait_ge(loaded, 7 * 16)

            @block.gpsimd
            def _(pool):
                pool.memset(v_pad[:, :, :, :], 0.0).then_inc(v_zero, 1)

            @block.tensor
            def _(pe):
                pe.wait_ge(loaded, 7 * 16)

                def scores(i, s):
                    hp, qt = s // 2, s % 2
                    if s >= 3:
                        pe.wait_ge(exp_done, i * 2 * NS + 2 * (s - 2))
                    u, r = hp // 4, 2 * hp % HPT
                    pe.matmul(SC[s % 3], qT[:, u, qt * P:(qt + 1) * P], kT[:, u, r:r + 2, :],
                              start=True, stop=True).then_inc(scores_done, 1)

                def turn_probs(i, s):
                    qt = s % 2
                    pe.wait_ge(probs_done, i * 2 * NS + 2 * (s + 1))
                    if s >= 2:
                        pe.wait_ge(diag_done, i * NS + s - 1)
                        if s >= 3:
                            pe.wait_ge(full_done, i * (NS // 2) + (s - 1) // 2)
                    for h in range(2):
                        for c in range(qt + 1):
                            last = pe.transpose(TR[s % 2][:, h, c, :], probs[:, s % 3, h, c * P:(c + 1) * P],
                                                ident[:, :])
                    last.then_inc(probsT_in_psum, 1)

                def weigh_values(i, hp):
                    u = hp // 4
                    pe.wait_ge(diag_done, i * NS + 2 * hp + 2)
                    pe.wait_ge(full_done, i * (NS // 2) + hp + 1)
                    for h in range(2):
                        r = (2 * hp + h) % HPT
                        for c in range(2):
                            last = pe.matmul(OT[u][:, c * P:T], v_pad[:, c, u, r * P:(r + 1) * P],
                                             probsT[:, hp % 2, h, c, c * P:T],
                                             start=(r == 0 and c == 0), stop=(r == HPT - 1 and c == 1),
                                             skip_group_check=True)
                    last.then_inc(av_done, 1)

                with pe.Fori(0, B) as i:
                    pe.wait_ge(xn_done, i * 2 + 2)
                    for n in range(2):
                        for c in range(KC):
                            last = pe.transpose(TA[:, (c * 2 + n) * P:(c * 2 + n + 1) * P],
                                                xn[:, n, c * P:(c + 1) * P], ident[:, :])
                    last.then_inc(xT_in_psum, 1)
                    pe.wait_ge(xT_done, i + 1)
                    for n in range(2):
                        for c in range(KC):
                            last = pe.matmul(PS[:, n, :], xT[:, c, n * P:(n + 1) * P], w_qkv[:, c, 0:2 * H],
                                             start=(c == 0), stop=(c == KC - 1))
                        last.then_inc(qkv_in_psum, 1)
                    for n in range(2):
                        for c in range(KC):
                            last = pe.matmul(PS[:, 2, n * H:(n + 1) * H], xT[:, c, n * P:(n + 1) * P],
                                             w_qkv[:, c, 2 * H:3 * H], start=(c == 0), stop=(c == KC - 1))
                    last.then_inc(qkv_in_psum, 1)
                    pe.wait_ge(rope_done, i * 2 + 2)
                    for part in range(2):
                        for n in range(2):
                            for u in range(2):
                                last = pe.transpose(TR[part][:, u, n, :],
                                                    qk[:, n, part * H + u * P:part * H + (u + 1) * P],
                                                    ident[:, :])
                        last.then_inc(qkT_in_psum, 1)
                    pe.wait_ge(qT_done, i + 1)
                    pe.wait_ge(kT_done, i * 2 + 2)
                    for s in range(NS + 4):
                        if s < NS:
                            scores(i, s)
                        if 2 <= s < NS + 2:
                            turn_probs(i, s - 2)
                        if s >= 4 and s % 2 == 0:
                            weigh_values(i, (s - 4) // 2)
                    pe.wait_ge(oT_done, i * 2 + 2)
                    for n in range(2):
                        for c in range(KC):
                            last = pe.matmul(YB[:, n, :], oT[:, c, n * P:(n + 1) * P], w_o[:, c, :],
                                             start=(c == 0), stop=(c == KC - 1))
                    last.then_inc(y_in_psum, 1)

            @block.scalar
            def _(act):
                def exps(i, s):
                    act.wait_ge(max_done, i * NS + s + 1)
                    if s >= 3:
                        act.wait_ge(probsT_in_psum, i * NS + s - 2)
                    for h in range(2):
                        nc.scalar.activation(probs[:, s % 3, h, :], SC[s % 3][:, h, :], ACT.Exp,
                                             bias=neg_max[:, s % 4, h:h + 1],
                                             accum_out=row_sum[:, s % 4, h:h + 1]).then_inc(exp_done, 1)

                def full_block(i, hp):
                    act.wait_ge(diag_done, i * NS + 2 * hp + 2)
                    if hp >= 2:
                        act.wait_ge(av_done, i * (NS // 2) + hp - 1)
                    nc.scalar.copy(probsT[:, hp % 2, :, 0, P:T], TR[1][:, :, 0, :]).then_inc(full_done, 1)

                act.wait_ge(mv_done, NT)
                nc.scalar.activation(std[:, :], mv[:, :, 1], ACT.Sqrt, bias=k.eps[:, 0:1]).then_inc(std_done, 1)
                with act.Fori(0, B) as i:
                    act.wait_ge(xT_in_psum, i + 1)
                    nc.scalar.copy(xT[:, :, :], TA.rearrange("p (c t) -> p c t", c=KC)).then_inc(xT_done, 1)
                    act.wait_ge(qkT_in_psum, i * 2 + 1)
                    nc.scalar.copy(qT[:, :, :], TR[0].rearrange("p u n t -> p u (n t)")).then_inc(qT_done, 1)
                    for s in range(NS + 2):
                        if s < NS:
                            exps(i, s)
                        if s >= 3 and s % 2:
                            full_block(i, (s - 3) // 2)
                        if s == 11:
                            act.wait_ge(av_done, i * (NS // 2) + 4)
                            nc.scalar.copy(oT[:, 0, :], OT[0]).then_inc(oT_done, 1)
                    act.wait_ge(av_done, i * (NS // 2) + 8)
                    nc.scalar.copy(oT[:, 1, :], OT[1]).then_inc(oT_done, 1)

            @block.vector
            def _(dve):
                dve.wait_ge(loaded, 7 * 16)
                dve.wait_ge(v_zero, 1)

                def row_max(i, s):
                    dve.wait_ge(scores_done, i * NS + s + 1)
                    nc.vector.tensor_reduce(neg_max[:, s % 4, :], SC[s % 3], AX.X, ALU.max, negate=True)\
                        .then_inc(max_done, 1)

                def normalise(i, s):
                    dve.wait_ge(exp_done, i * 2 * NS + 2 * (s + 1))
                    nc.vector.reciprocal(row_inv[:, s % 4, :], row_sum[:, s % 4, :]).then_inc(inv_done, 1)
                    dve.wait_ge(inv_done, i * NS + s + 1)
                    for h in range(2):
                        p = probs[:, s % 3, h, :]
                        nc.vector.tensor_scalar(p, p, row_inv[:, s % 4, h:h + 1], None, ALU.mult)\
                            .then_inc(probs_done, 1)

                def diag_block(i, s):
                    hp, qt = s // 2, s % 2
                    dve.wait_ge(probsT_in_psum, i * NS + s + 1)
                    if hp >= 2 and qt == 0:
                        dve.wait_ge(av_done, i * (NS // 2) + hp - 1)
                    nc.vector.tensor_tensor(probsT[:, hp % 2, :, qt, qt * P:(qt + 1) * P],
                                            TR[s % 2][:, :, qt, :], bc(k.tri_incl[:, :], 1, 2), ALU.mult)\
                        .then_inc(diag_done, 1)

                for n in range(NT):
                    nc.vector.bn_stats(stats[:, n, :], X[:, n, :]).then_inc(stats_done, 1)
                dve.wait_ge(stats_done, NT)
                for n in range(NT):
                    nc.vector.bn_aggr(mv[:, n, :], stats[:, n, :]).then_inc(mv_done, 1)
                dve.wait_ge(std_done, 1)
                nc.vector.reciprocal(rstd[:, :], std[:, :]).then_inc(rstd_done, 1)
                dve.wait_ge(rstd_done, 1)
                with dve.Fori(0, B) as i:
                    for n in range(2):
                        t = bass.ds(2 * i + n, 1)
                        nc.vector.tensor_scalar(xn[:, n, :], X[:, t, :], mv[:, t, 0], rstd[:, t],
                                                ALU.subtract, ALU.mult).then_inc(xn_done, 1)
                    for n in range(2):
                        dve.wait_ge(qkv_in_psum, i * 3 + n + 1)
                        nc.vector.tensor_tensor(qk[:, n, :], PS[:, n, :], b_qkv[:, 0:2 * H], ALU.add)\
                            .then_inc(qk_done, 1)
                    dve.wait_ge(qkv_in_psum, i * 3 + 3)
                    for n in range(2):
                        for u in range(2):
                            c0 = 2 * H + u * P
                            dst = v_pad[:, n, u, :].rearrange("p (r c) -> p r c", c=VPITCH)[:, :, 0:HSA]
                            nc.vector.tensor_tensor(
                                dst, PS[:, 2, n * H + u * P:n * H + (u + 1) * P].rearrange("p (r c) -> p r c", c=HSA),
                                b_qkv[:, c0:c0 + P].rearrange("p (r c) -> p r c", c=HSA), ALU.add).then_inc(qk_done, 1)
                    dve.wait_ge(qk_done, i * 6 + 2)
                    for n in range(2):
                        heads = qk[:, n, :].rearrange("p (a h c) -> p a h c", a=2, c=HSA)
                        for a in range(2):
                            nc.vector.tensor_tensor(
                                qk_cos[:, n, a * H:(a + 1) * H].rearrange("p (h c) -> p h c", c=HSA),
                                heads[:, a], bc(cos[:, n, a, :], 1, NHA), ALU.mult).then_inc(rope_parts, 1)
                            for e in range(2):
                                out = qk_sin[:, n, a * H:(a + 1) * H].rearrange("p (h e c) -> p h e c", e=2, c=8)
                                nc.vector.tensor_tensor(
                                    out[:, :, e, :], heads[:, a, :, (1 - e) * 8:(2 - e) * 8],
                                    bc(sin[:, n, a, e * 8:(e + 1) * 8], 1, NHA), ALU.mult).then_inc(rope_parts, 1)
                    for n in range(2):
                        dve.wait_ge(rope_parts, i * 12 + 6 * (n + 1))
                        nc.vector.tensor_tensor(qk[:, n, :], qk_cos[:, n, :], qk_sin[:, n, :], ALU.add)\
                            .then_inc(rope_done, 1)
                    dve.wait_ge(qkT_in_psum, i * 2 + 2)
                    for u in range(2):
                        nc.vector.tensor_tensor(
                            kT[:, u, :, :], bc(TR[1][:, u].rearrange("p n t -> p (n t)"), 1, HPT),
                            bc(head_rows[:, :], 2, T), ALU.mult).then_inc(kT_done, 1)
                    for s in range(NS + 2):
                        if s < NS:
                            row_max(i, s)
                        if 1 <= s < NS + 1:
                            normalise(i, s - 1)
                        if s >= 2:
                            diag_block(i, s - 2)
                    dve.wait_ge(y_in_psum, i + 1)
                    nc.vector.tensor_tensor(y[:, :, :], YB, bc(b_o[:, :], 1, 2), ALU.add).then_inc(y_done, 1)
                    dve.wait_ge(y_done, i + 1)
                    xs = X[:, bass.ds(2 * i, 2), :]
                    nc.vector.tensor_tensor(xs, xs, y[:, :, :], ALU.add).then_inc(x_done, 1)
                    dve.wait_ge(x_done, i + 1)


def stage_moe(k, I_, run, bufs, outs):
    nc, X, ident, PS = k.nc, k.X, k.ident, k.PS
    EG = 4
    with semaphores(nc) as take, ExitStack() as ctx:
        def sb(name, shape, dt=F32):
            return ctx.enter_context(nc.sbuf_tensor(f"m{run}_{name}", shape, dt))

        def sem(name):
            return take(f"m{run}_{name}")

        xn = sb("xn", [P, NT, H])
        xT = sb("xT", [P, KC, B * T])
        w_router = sb("w_router", [P, KC, E])
        w_sg = sb("w_sg", [P, KC, IS])
        w_su = sb("w_su", [P, KC, IS])
        w_sd = sb("w_sd", [P, len(SHC), H])
        w_gu = sb("w_gu", [P, EG, KC * 2 * I])
        w_d = sb("w_d", [IH, EG, 2 * H])
        top_w = sb("top_w", [P, NT, 8])
        slot_in = sb("slot_in", [P, 2, NT], U32)
        slot_out = sb("slot_out", [P, 2, NT], U32)

        xT_done = sem("xT_done")
        shared_loaded = sem("shared_loaded")
        scattered = sem("scattered")
        gu_loaded = [sem(f"gu_loaded{j}") for j in range(EG)]
        d_loaded = [sem(f"d_loaded{j}") for j in range(EG)]

        def load_experts(sp, g, up_done, down_done):
            for j in range(EG):
                if up_done is not None:
                    sp.wait_ge(up_done, g * EG - EG + j + 1)
                sp.dma_start(w_gu[:, j:j + 1, :], I_["m_w_gu"].rearrange("e p n -> p e n")[:, bass.ds(g * EG + j, 1), :])\
                    .then_inc(gu_loaded[j], 16)
                if down_done is not None:
                    sp.wait_ge(down_done, g * EG - EG + j + 1)
                sp.dma_start(w_d[:, j:j + 1, :], I_["m_w_d"].rearrange("e p n -> p e n")[:, bass.ds(g * EG + j, 1), :])\
                    .then_inc(d_loaded[j], 16)

        with ExitStack() as c1:
            def sb1(name, shape, dt=F32):
                return c1.enter_context(nc.sbuf_tensor(f"m{run}_{name}", shape, dt))

            def sem1(name):
                return take(f"m{run}_{name}")

            stats = sb1("stats", [P, NT, 6])
            mv = sb1("mv", [P, NT, 2])
            std = sb1("std", [P, NT])
            rstd = sb1("rstd", [P, NT])
            expert_no = sb1("expert_no", [P, E])
            strict = sb1("strict", [P, P], BF16)
            ones = sb1("ones", [P, P], BF16)
            neg_max = sb1("neg_max", [P, NT])
            shifted = sb1("shifted", [P, NT, E])
            ex = sb1("ex", [P, NT, E])
            total = sb1("total", [P, NT])
            inv = sb1("inv", [P, NT])
            scores = sb1("scores", [P, NT, E])
            top_i = sb1("top_i", [P, NT, 8], U32)
            top_f = sb1("top_f", [P, 2, NT])
            chosen = sb1("chosen", [P, 2, NT, E])
            either = sb1("either", [P, NT, E], BF16)
            rank_of = sb1("rank_of", [P, 2, NT, E])
            rank = sb1("rank", [P, 2, NT])
            over = sb1("over", [P, 2, NT])
            far = sb1("far", [P, 2, NT])
            held = sb1("held", [P, 2, NT])

            router_loaded = sem1("router_loaded")
            const_ready = sem1("const_ready")
            stats_done = sem1("stats_done")
            mv_done = sem1("mv_done")
            std_done = sem1("std_done")
            rstd_done = sem1("rstd_done")
            xn_done = sem1("xn_done")
            xT_in_psum = sem1("xT_in_psum")
            logits_done = sem1("logits_done")
            exp_done = sem1("exp_done")
            step = sem1("route_step")
            either_done = sem1("either_done")
            rank_in_psum = sem1("rank_in_psum")
            slots_done = sem1("slots_done")

            LG = PS[:, 4, 0:NT * E].rearrange("p (n e) -> p n e", e=E)
            RK = PS[:, 5, 0:NT * E].rearrange("p (n e) -> p n e", e=E)

            with nc.Block() as block:

                @block.sync
                def _(sp):
                    sp.dma_start(w_router[:, :, :], I_["m_w_router"]).then_inc(router_loaded, 16)
                    sp.dma_start(expert_no[:, :], I_["m_expert_no"]).then_inc(router_loaded, 16)
                    for dst, name in ((w_sg, "m_w_sg"), (w_su, "m_w_su"), (w_sd, "m_w_sd")):
                        sp.dma_start(dst[:, :, :], I_[name]).then_inc(shared_loaded, 16)
                    load_experts(sp, 0, None, None)
                    sp.wait_ge(router_loaded, 32)

                @block.tensor
                def _(pe):
                    for n in range(NT):
                        pe.wait_ge(xn_done, n + 1)
                        if n % 2 == 0:
                            bank = PS[:, n // 2 % 4, :].rearrange("p (c t) -> p c t", c=KC)
                        for c in range(KC):
                            last = pe.transpose(bank[:, c, n % 2 * P:(n % 2 + 1) * P],
                                                xn[:, n, c * P:(c + 1) * P], ident[:, :])
                        last.then_inc(xT_in_psum, 1)
                    pe.wait_ge(router_loaded, 32)
                    for n in range(NT):
                        if n % 2 == 0:
                            pe.wait_ge(xT_done, n // 2 + 1)
                        for c in range(KC):
                            last = pe.matmul(LG[:, n, :], xT[:, c, n * P:(n + 1) * P], w_router[:, c, :],
                                             start=(c == 0), stop=(c == KC - 1))
                    last.then_inc(logits_done, 1)
                    pe.wait_ge(const_ready, 2)
                    pe.wait_ge(either_done, 1)
                    flat = either[:, :, :].rearrange("p n e -> p (n e)")
                    out = RK.rearrange("p n e -> p (n e)")
                    last = pe.matmul(out, strict[:, :], flat, start=True, stop=False, skip_group_check=True)
                    for m in range(1, NT):
                        last = pe.matmul(out[:, m * E:NT * E], ones[:, :], flat[:, 0:(NT - m) * E],
                                         start=False, stop=(m == NT - 1), skip_group_check=True)
                    last.then_inc(rank_in_psum, 1)

                @block.scalar
                def _(act):
                    act.wait_ge(mv_done, NT)
                    nc.scalar.activation(std[:, :], mv[:, :, 1], ACT.Sqrt, bias=k.eps[:, 0:1])\
                        .then_inc(std_done, 1)
                    for g in range(NT // 2):
                        act.wait_ge(xT_in_psum, 2 * g + 2)
                        nc.scalar.copy(xT[:, :, 2 * g * P:2 * (g + 1) * P],
                                       PS[:, g % 4, :].rearrange("p (c t) -> p c t", c=KC)).then_inc(xT_done, 1)
                    act.wait_ge(step, 2)
                    nc.scalar.activation(ex[:, :, :], shifted[:, :, :], ACT.Exp).then_inc(exp_done, 1)

                @block.vector
                def _(dve):
                    for n in range(NT):
                        nc.vector.bn_stats(stats[:, n, :], X[:, n, :]).then_inc(stats_done, 1)
                    dve.wait_ge(stats_done, NT)
                    for n in range(NT):
                        nc.vector.bn_aggr(mv[:, n, :], stats[:, n, :]).then_inc(mv_done, 1)
                    dve.wait_ge(std_done, 1)
                    nc.vector.reciprocal(rstd[:, :], std[:, :]).then_inc(rstd_done, 1)
                    dve.wait_ge(rstd_done, 1)
                    for n in range(NT):
                        nc.vector.tensor_scalar(xn[:, n, :], X[:, n, :], mv[:, n, 0:1], rstd[:, n:n + 1],
                                                ALU.subtract, ALU.mult).then_inc(xn_done, 1)
                    nc.vector.tensor_copy(strict[:, :], k.tri_strict[:, :]).then_inc(const_ready, 1)
                    dve.wait_ge(logits_done, 1)
                    nc.vector.tensor_reduce(neg_max[:, :], LG, AX.X, ALU.max, negate=True).then_inc(step, 1)
                    dve.wait_ge(step, 1)
                    nc.vector.tensor_tensor(shifted[:, :, :], LG, bc(neg_max[:, :], 2, E), ALU.add).then_inc(step, 1)
                    dve.wait_ge(exp_done, 1)
                    nc.vector.tensor_reduce(total[:, :], ex[:, :, :], AX.X, ALU.add).then_inc(step, 1)
                    dve.wait_ge(step, 3)
                    nc.vector.reciprocal(inv[:, :], total[:, :]).then_inc(step, 1)
                    dve.wait_ge(step, 4)
                    nc.vector.tensor_tensor(scores[:, :, :], ex[:, :, :], bc(inv[:, :], 2, E), ALU.mult).then_inc(step, 1)
                    dve.wait_ge(step, 5)
                    for n in range(NT):
                        nc.vector.max(top_w[:, n, :], scores[:, n, :]).then_inc(step, 1)
                    for n in range(NT):
                        dve.wait_ge(step, 6 + n)
                        nc.vector.max_index(top_i[:, n, :], top_w[:, n, :], scores[:, n, :]).then_inc(step, 1)
                    dve.wait_ge(step, 21)
                    nc.vector.tensor_copy(top_f[:, :, :], top_i[:, :, 0:2].rearrange("p n k -> p k n"))\
                        .then_inc(step, 1)
                    dve.wait_ge(step, 22)
                    dve.wait_ge(router_loaded, 32)
                    for q in range(2):
                        nc.vector.tensor_tensor(chosen[:, q], bc(expert_no[:, :], 1, NT), bc(top_f[:, q, :], 2, E),
                                                ALU.is_equal).then_inc(step, 1)
                    dve.wait_ge(step, 24)
                    nc.vector.tensor_tensor(either[:, :, :], chosen[:, 0], chosen[:, 1], ALU.add)\
                        .then_inc(either_done, 1)
                    dve.wait_ge(rank_in_psum, 1)
                    for q in range(2):
                        nc.vector.tensor_tensor(rank_of[:, q], RK, chosen[:, q], ALU.mult).then_inc(step, 1)
                    dve.wait_ge(step, 26)
                    nc.vector.tensor_reduce(rank[:, :, :], rank_of[:, :, :, :], AX.X, ALU.add).then_inc(step, 1)
                    dve.wait_ge(step, 27)
                    nc.vector.tensor_scalar(over[:, :, :], rank[:, :, :], float(CAP), float(2 * E * CAP),
                                            ALU.is_ge, ALU.mult).then_inc(step, 1)
                    nc.vector.tensor_scalar(held[:, :, :], rank[:, :, :], float(CAP - 1), None, ALU.min)\
                        .then_inc(step, 1)
                    dve.wait_ge(step, 28)
                    nc.vector.tensor_tensor(far[:, :, :], rank[:, :, :], over[:, :, :], ALU.add).then_inc(step, 1)
                    dve.wait_ge(step, 30)
                    for dst, r in ((slot_in, far), (slot_out, held)):
                        nc.vector.scalar_tensor_tensor(out=dst[:, :, :], in0=top_f[:, :, :], scalar=float(CAP),
                                                       in1=r[:, :, :], op0=ALU.mult, op1=ALU.add)\
                            .then_inc(slots_done, 1)

                @block.gpsimd
                def _(pool):
                    pool.memset(ones[:, :], 1.0).then_inc(const_ready, 1)
                    pool.wait_ge(slots_done, 1)
                    for q in range(2):
                        for n in range(NT):
                            pool.indirect_dma_start(
                                out=bufs[:, :], out_offset=bass.IndirectOffsetOnAxis(ap=slot_in[:, q, n:n + 1], axis=0),
                                in_=xn[:, n, :], in_offset=None, bounds_check=E * CAP - 1,
                                oob_is_err=False).then_inc(scattered, 16)
                    pool.wait_ge(scattered, 16 * 2 * NT)

        with ExitStack() as c2:
            def sb2(name, shape, dt=F32):
                return c2.enter_context(nc.sbuf_tensor(f"m{run}_{name}", shape, dt))

            def sem2(name):
                return take(f"m{run}_{name}")

            TH = 4 * P
            s_gate = sb2("s_gate", [P, 2, TH])
            s_h = sb2("s_h", [P, len(SHC), TH])
            rows = sb2("rows", [P, EG, H])
            rowsT = sb2("rowsT", [P, EG, KC, CAP])
            gate = sb2("gate", [P, EG, I])
            hid = sb2("hid", [P, EG, I])
            hidT = sb2("hidT", [IH, EG, 2, CAP])
            res = sb2("res", [P, EG, H])

            s_up_done = sem2("s_up_done")
            s_silu_done = sem2("s_silu_done")
            s_h_done = sem2("s_h_done")
            s_y_done = sem2("s_y_done")
            s_x_done = sem2("s_x_done")
            rows_loaded = [sem2(f"rows_loaded{j}") for j in range(EG)]
            rowsT_in_psum = sem2("rowsT_in_psum")
            rowsT_done = sem2("rowsT_done")
            up_done = sem2("up_done")
            silu_done = sem2("silu_done")
            hid_done = sem2("hid_done")
            hidT_in_psum = sem2("hidT_in_psum")
            hidT_done = sem2("hidT_done")
            down_done = sem2("down_done")
            res_done = sem2("res_done")
            stored = [sem2(f"stored{j}") for j in range(EG)]

            SG, SU = PS[:, 0, :], PS[:, 1, :]
            SG2, SU2 = PS[:, 2, :], PS[:, 3, :]
            UP = [(SG, SU), (SG2, SU2)]
            NCH = len(SHC)
            with nc.Block() as block:

                @block.sync
                def _(sp):
                    def load_rows(g, j):
                        sp.dma_start(rows[:, j, :], bufs[bass.ds((g * EG + j) * CAP, CAP), :])\
                            .then_inc(rows_loaded[j], 16)

                    def store(g, j):
                        sp.wait_ge(res_done, EG + g * EG + j + 1)
                        sp.dma_start(outs[bass.ds((g * EG + j) * CAP, CAP), :], res[:, j, :])\
                            .then_inc(stored[j], 16)

                    for j in range(EG):
                        load_rows(0, j)
                        sp.sem_inc(stored[j], 16)
                    with sp.Fori(1, E // EG) as step_no:
                        g = sp.snap(step_no)
                        for j in range(EG):
                            sp.wait_ge(rowsT_in_psum, g * EG - EG + j + 1)
                            load_rows(g, j)
                        load_experts(sp, g, up_done, down_done)
                        for j in range(EG):
                            store(g - 1, j)
                    for j in range(EG):
                        store(E // EG - 1, j)
                    for j in range(EG):
                        sp.wait_ge(stored[j], 16 + 16 * E // EG)

                @block.tensor
                def _(pe):
                    pe.wait_ge(shared_loaded, 48)
                    with pe.Fori(0, NT * P // TH) as h:
                        for q, (c0, m) in enumerate(SHC):
                            if q >= 2:
                                pe.wait_ge(s_h_done, h * NCH + q - 1)
                            for w, bank in zip((w_sg, w_su), UP[q % 2]):
                                for c in range(KC):
                                    last = pe.matmul(bank[0:m, :], w[:, c, c0:c0 + m],
                                                     xT[:, c, bass.ds(h * TH, TH)],
                                                     start=(c == 0), stop=(c == KC - 1))
                            last.then_inc(s_up_done, 1)
                        pe.wait_ge(s_h_done, h * NCH + NCH)
                        for n in range(4):
                            for q, (c0, m) in enumerate(SHC):
                                last = pe.matmul(PS[:, 4 + n // 2, n % 2 * H:(n % 2 + 1) * H],
                                                 s_h[0:m, q, n * P:(n + 1) * P], w_sd[0:m, q, :],
                                                 start=(q == 0), stop=(q == NCH - 1))
                            if n % 2:
                                last.then_inc(s_y_done, 1)
                    with pe.Fori(0, E // EG) as g:
                        for j in range(EG):
                            pe.wait_ge(rows_loaded[j], g * 16 + 16)
                            if j == 0:
                                pe.wait_ge(s_x_done, 2 * NT * P // TH)
                            pe.wait_ge(res_done, g * EG + j + 1)
                            for c in range(KC):
                                last = pe.transpose(PS[:, 4 + j, c * P:(c + 1) * P],
                                                    rows[:, j, c * P:(c + 1) * P], ident[:, :])
                            last.then_inc(rowsT_in_psum, 1)
                        for j in range(EG):
                            pe.wait_ge(rowsT_done, g * EG + j + 1)
                            pe.wait_ge(gu_loaded[j], g * 16 + 16)
                            for c in range(KC):
                                last = pe.matmul(PS[:, j, 0:2 * I], rowsT[:, j, c, :], w_gu[:, j, c * 2 * I:(c + 1) * 2 * I],
                                                 start=(c == 0), stop=(c == KC - 1))
                            last.then_inc(up_done, 1)
                        for j in range(EG):
                            pe.wait_ge(hid_done, g * EG + j + 1)
                            for c in range(2):
                                last = pe.transpose(PS[0:IH, 4 + j, c * P:(c + 1) * P],
                                                    hid[:, j, c * IH:(c + 1) * IH], ident[:, :])
                            last.then_inc(hidT_in_psum, 1)
                        for j in range(EG):
                            pe.wait_ge(hidT_done, g * EG + j + 1)
                            pe.wait_ge(d_loaded[j], g * 16 + 16)
                            for c in range(2):
                                last = pe.matmul(PS[:, 4 + j, H:2 * H], hidT[:, j, c, :], w_d[:, j, c * H:(c + 1) * H],
                                                 start=(c == 0), stop=(c == 1))
                            last.then_inc(down_done, 1)

                @block.scalar
                def _(act):
                    with act.Fori(0, NT * P // TH) as h:
                        for q, (c0, m) in enumerate(SHC):
                            act.wait_ge(s_up_done, h * NCH + q + 1)
                            nc.scalar.activation(s_gate[0:m, q % 2, :], UP[q % 2][0][0:m, :], ACT.Silu)\
                                .then_inc(s_silu_done, 1)
                            if q:
                                act.wait_ge(s_h_done, h * NCH + q)
                    with act.Fori(0, E // EG) as g:
                        for j in range(EG):
                            act.wait_ge(rowsT_in_psum, g * EG + j + 1)
                            nc.scalar.copy(rowsT[:, j, :, :],
                                           PS[:, 4 + j, 0:H].rearrange("p (c t) -> p c t", c=KC)).then_inc(rowsT_done, 1)
                        for j in range(EG):
                            act.wait_ge(up_done, g * EG + j + 1)
                            nc.scalar.activation(gate[:, j, :], PS[:, j, 0:I], ACT.Silu).then_inc(silu_done, 1)
                        for j in range(EG):
                            act.wait_ge(hidT_in_psum, g * EG + j + 1)
                            nc.scalar.copy(hidT[:, j, :, :],
                                           PS[0:IH, 4 + j, 0:2 * P].rearrange("p (c t) -> p c t", c=2))\
                                .then_inc(hidT_done, 1)

                @block.vector
                def _(dve):
                    with dve.Fori(0, NT * P // TH) as h:
                        for q, (c0, m) in enumerate(SHC):
                            dve.wait_ge(s_silu_done, h * NCH + q + 1)
                            nc.vector.tensor_tensor(s_h[0:m, q, :], s_gate[0:m, q % 2, :], UP[q % 2][1][0:m, :],
                                                    ALU.mult).then_inc(s_h_done, 1)
                        for n in range(2):
                            dve.wait_ge(s_y_done, h * 2 + n + 1)
                            xs = X[:, bass.ds(h * 4 + 2 * n, 2), :]
                            nc.vector.tensor_tensor(xs, xs, PS[:, 4 + n, :].rearrange("p (n d) -> p n d", n=2),
                                                    ALU.add).then_inc(s_x_done, 1)
                    dve.sem_inc(res_done, EG)
                    with dve.Fori(0, E // EG) as g:
                        for j in range(EG):
                            dve.wait_ge(silu_done, g * EG + j + 1)
                            nc.vector.tensor_tensor(hid[:, j, :], gate[:, j, :], PS[:, j, I:2 * I], ALU.mult)\
                                .then_inc(hid_done, 1)
                        for j in range(EG):
                            dve.wait_ge(down_done, g * EG + j + 1)
                            dve.wait_ge(stored[j], g * 16 + 16)
                            nc.vector.tensor_copy(res[:, j, :], PS[:, 4 + j, H:2 * H]).then_inc(res_done, 1)

        with ExitStack() as c3:
            got = c3.enter_context(nc.sbuf_tensor(f"m{run}_got", [P, NT, 2, H], F32))
            gathered = [take(f"m{run}_gathered{n}") for n in range(NT)]
            first_added = take(f"m{run}_first_added")
            second_added = take(f"m{run}_second_added")
            def second(dve, n):
                dve.wait_ge(first_added, n + 1)
                nc.vector.scalar_tensor_tensor(out=X[:, n, :], in0=got[:, n, 1, :], scalar=top_w[:, n, 1:2],
                                               in1=X[:, n, :], op0=ALU.mult, op1=ALU.add)\
                    .then_inc(second_added, 1)

            with nc.Block() as block:

                @block.gpsimd
                def _(pool):
                    for n in range(NT):
                        for q in range(2):
                            pool.indirect_dma_start(
                                out=got[:, n, q, :], out_offset=None, in_=outs[:, :],
                                in_offset=bass.IndirectOffsetOnAxis(ap=slot_out[:, q, n:n + 1], axis=0),
                                bounds_check=E * CAP - 1, oob_is_err=True).then_inc(gathered[n], 16)
                    for n in range(NT):
                        pool.wait_ge(gathered[n], 32)

                @block.vector
                def _(dve):
                    for n in range(NT):
                        dve.wait_ge(gathered[n], 32)
                        nc.vector.scalar_tensor_tensor(out=X[:, n, :], in0=got[:, n, 0, :], scalar=top_w[:, n, 0:1],
                                                       in1=X[:, n, :], op0=ALU.mult, op1=ALU.add)\
                            .then_inc(first_added, 1)
                        if n:
                            second(dve, n - 1)
                    second(dve, NT - 1)


LEVELS = [2, 4, 8, 16, 32, 64]
NG = 4
WPAIR = KC * 4 * P + 3 * TAPS


def stage_delta(k, I_):
    nc, X, ident, PS = k.nc, k.X, k.ident, k.PS
    NL = len(LEVELS)
    with semaphores(nc) as take, ExitStack() as ctx:
        def sb(name, shape, dt=F32):
            return ctx.enter_context(nc.sbuf_tensor("d_" + name, shape, dt))

        def sem(name):
            return take("d_" + name)

        xT = sb("xT", [P, KC, B * T])
        w_pair = sb("w_pair", [P, WPAIR])
        w_out = sb("w_out", [P, H])
        off_mask = sb("off_mask", [P, NL, P])
        pair_mask = sb("pair_mask", [P, P])
        after = sb("after", [P, P])
        neg_half = sb("neg_half", [P, 16])
        norm_eps = sb("norm_eps", [P, 16])
        o_eps = sb("o_eps", [P, 16])
        gate_w = sb("gate_w", [P, 1])
        beta = sb("beta", [P, NH, NT])
        g = sb("g", [P, NH, NT])
        grow = sb("grow", [P, NH, NT])
        rest = sb("rest", [P, NH, NT])

        setup_loaded = sem("setup_loaded")
        w_loaded = sem("w_loaded")
        wo_loaded = sem("wo_loaded")

        def w_src(p):
            return I_["d_w_pair"].rearrange("q p n -> p q n")[:, bass.ds(p, 1), :]

        def wo_src(p):
            return I_["d_w_out"].rearrange("q p n -> p q n")[:, bass.ds(p, 1), :]

        with ExitStack() as c1:
            def sb1(name, shape, dt=F32):
                return c1.enter_context(nc.sbuf_tensor("d_" + name, shape, dt))

            def sem1(name):
                return take("d_" + name)

            stats = sb1("stats", [P, NT, 6])
            mv = sb1("mv", [P, NT, 2])
            std = sb1("std", [P, NT])
            rstd = sb1("rstd", [P, NT])
            xn = sb1("xn", [P, NT, H])
            w_ba = sb1("w_ba", [P, KC, 2 * NH])
            a_log = sb1("a_log", [P, NH])
            dt_bias = sb1("dt_bias", [P, NH])
            norm_w = sb1("norm_w", [P, 1])
            exp_a = sb1("exp_a", [P, NH])
            s_in = sb1("s_in", [P, NT, NH])
            s_abs = sb1("s_abs", [P, NT, NH])
            s_exp = sb1("s_exp", [P, NT, NH])
            s_ln = sb1("s_ln", [P, NT, NH])
            soft = sb1("soft", [P, NT, NH])
            half_tanh = sb1("half_tanh", [P, NT, NH])

            stats_done = sem1("stats_done")
            mv_done = sem1("mv_done")
            std_done = sem1("std_done")
            rstd_done = sem1("rstd_done")
            xn_done = sem1("xn_done")
            xT_in_psum = sem1("xT_in_psum")
            xT_done = sem1("xT_done")
            ba_done = sem1("ba_done")
            gate_act = sem1("gate_act")
            gate_dve = sem1("gate_dve")
            sums_done = sem1("sums_done")
            BA = PS[:, 4, :].rearrange("p (n c) -> p n c", n=NT)

            with nc.Block() as block:

                @block.sync
                def _(sp):
                    sp.dma_start(w_ba[:, :, :], I_["d_w_ba"]).then_inc(setup_loaded, 16)
                    sp.dma_start(a_log[:, :], I_["d_a_log"].partition_broadcast(P)).then_inc(setup_loaded, 16)
                    sp.dma_start(dt_bias[:, :], I_["d_dt_bias"].partition_broadcast(P)).then_inc(setup_loaded, 16)
                    sp.dma_start(norm_w[:, :], I_["d_norm_w"]).then_inc(setup_loaded, 16)
                    sp.dma_start(after[:, :], I_["after"]).then_inc(setup_loaded, 16)
                    sp.dma_start(pair_mask[:, :], I_["pair_mask"]).then_inc(setup_loaded, 16)
                    sp.dma_start(off_mask[:, :, :], I_["off_mask"]).then_inc(setup_loaded, 16)
                    sp.wait_ge(setup_loaded, 7 * 16)

                @block.gpsimd
                def _(pool):
                    pool.memset(neg_half[:, :], -0.5)
                    pool.memset(norm_eps[:, 0:8], D * GEPS)
                    pool.memset(norm_eps[:, 8:16], GEPS)
                    pool.memset(o_eps[:, :], GEPS)

                @block.tensor
                def _(pe):
                    for n in range(NT):
                        pe.wait_ge(xn_done, n + 1)
                        bank = PS[:, n // 2, :].rearrange("p (c t) -> p c t", c=KC)
                        for c in range(KC):
                            last = pe.transpose(bank[:, c, n % 2 * P:(n % 2 + 1) * P],
                                                xn[:, n, c * P:(c + 1) * P], ident[:, :])
                        last.then_inc(xT_in_psum, 1)
                    pe.wait_ge(setup_loaded, 7 * 16)
                    for n in range(NT):
                        if n % 2 == 0:
                            pe.wait_ge(xT_done, n // 2 + 1)
                        for c in range(KC):
                            last = pe.matmul(BA[:, n, :], xT[:, c, n * P:(n + 1) * P], w_ba[:, c, :],
                                             start=(c == 0), stop=(c == KC - 1))
                    last.then_inc(ba_done, 1)
                    pe.wait_ge(gate_dve, 5)
                    flat = g[:, :, :].rearrange("p h n -> p (h n)")
                    pe.matmul(PS[:, 5, 0:NH * NT], k.tri_incl[:, :], flat, start=True, stop=True)
                    pe.matmul(PS[:, 5, NH * NT:2 * NH * NT], after[:, :], flat, start=True, stop=True)\
                        .then_inc(sums_done, 1)

                @block.scalar
                def _(act):
                    act.wait_ge(mv_done, NT)
                    nc.scalar.activation(std[:, :], mv[:, :, 1], ACT.Sqrt, bias=k.eps[:, 0:1])\
                        .then_inc(std_done, 1)
                    for q in range(NT // 2):
                        act.wait_ge(xT_in_psum, 2 * q + 2)
                        nc.scalar.copy(xT[:, :, 2 * q * P:2 * (q + 1) * P],
                                       PS[:, q, :].rearrange("p (c t) -> p c t", c=KC)).then_inc(xT_done, 1)
                    act.wait_ge(setup_loaded, 7 * 16)
                    nc.scalar.activation(exp_a[:, :], a_log[:, :], ACT.Exp).then_inc(gate_act, 1)
                    act.wait_ge(ba_done, 1)
                    nc.scalar.activation(half_tanh[:, :, :], BA[:, :, 0:NH], ACT.Tanh, scale=0.5)\
                        .then_inc(gate_act, 1)
                    act.wait_ge(gate_dve, 2)
                    nc.scalar.activation(s_abs[:, :, :], s_in[:, :, :], ACT.Abs).then_inc(gate_act, 1)
                    act.wait_ge(gate_act, 3)
                    nc.scalar.activation(s_exp[:, :, :], s_abs[:, :, :], ACT.Exp, scale=-1.0).then_inc(gate_act, 1)
                    act.wait_ge(gate_act, 4)
                    nc.scalar.activation(s_ln[:, :, :], s_exp[:, :, :], ACT.Ln, bias=1.0).then_inc(gate_act, 1)
                    act.wait_ge(sums_done, 1)
                    nc.scalar.activation(grow[:, :, :], PS[:, 5, 0:NH * NT].rearrange("p (h n) -> p h n", n=NT),
                                         ACT.Exp)
                    nc.scalar.activation(rest[:, :, :],
                                         PS[:, 5, NH * NT:2 * NH * NT].rearrange("p (h n) -> p h n", n=NT), ACT.Exp)

                @block.vector
                def _(dve):
                    for n in range(NT):
                        nc.vector.bn_stats(stats[:, n, :], X[:, n, :]).then_inc(stats_done, 1)
                    dve.wait_ge(stats_done, NT)
                    for n in range(NT):
                        nc.vector.bn_aggr(mv[:, n, :], stats[:, n, :]).then_inc(mv_done, 1)
                    dve.wait_ge(std_done, 1)
                    nc.vector.reciprocal(rstd[:, :], std[:, :]).then_inc(rstd_done, 1)
                    dve.wait_ge(rstd_done, 1)
                    for n in range(NT):
                        nc.vector.tensor_scalar(xn[:, n, :], X[:, n, :], mv[:, n, 0:1], rstd[:, n:n + 1],
                                                ALU.subtract, ALU.mult).then_inc(xn_done, 1)
                    dve.wait_ge(setup_loaded, 7 * 16)
                    nc.vector.tensor_scalar(gate_w[:, :], norm_w[:, :], 0.5, None, ALU.mult).then_inc(gate_dve, 1)
                    dve.wait_ge(gate_act, 2)
                    nc.vector.tensor_tensor(s_in[:, :, :], BA[:, :, NH:2 * NH], bc(dt_bias[:, :], 1, NT), ALU.add)\
                        .then_inc(gate_dve, 1)
                    nc.vector.tensor_scalar(beta[:, :, :].rearrange("p h n -> p n h"), half_tanh[:, :, :], 0.5, 0.5,
                                            ALU.mult, ALU.add).then_inc(gate_dve, 1)
                    dve.wait_ge(gate_act, 5)
                    dve.wait_ge(gate_dve, 3)
                    nc.vector.scalar_tensor_tensor(out=soft[:, :, :], in0=s_in[:, :, :], scalar=0.0,
                                                   in1=s_ln[:, :, :], op0=ALU.max, op1=ALU.add).then_inc(gate_dve, 1)
                    dve.wait_ge(gate_dve, 4)
                    nc.vector.scalar_tensor_tensor(out=g[:, :, :].rearrange("p h n -> p n h"), in0=soft[:, :, :],
                                                   scalar=-1.0, in1=bc(exp_a[:, :], 1, NT), op0=ALU.mult,
                                                   op1=ALU.mult).then_inc(gate_dve, 1)

        pad = sb("pad", [P, 3, B, PADT])
        conv = sb("conv", [P, 3, B, T])
        w_gated = sb("w_gated", [P, H])
        z_tanh = sb("z_tanh", [P, NT, P])
        square = sb("square", [P, 2, 4, P])
        ssum = sb("ssum", [P, 4, 8])
        ssum_e = sb("ssum_e", [P, 4, 8])
        rnorm = sb("rnorm", [P, 4, 8])
        qk_tok = sb("qk_tok", [P, 2, NT, P])
        k_rest = sb("k_rest", [P, B, P])
        v_tok = sb("v_tok", [P, NT, P])
        qkT = sb("qkT", [P, B * T // P, 2, P])
        g_tri = sb("g_tri", [P, 2, B, P])
        decay = sb("decay", [P, 2, B, P])
        decay_incl = sb("decay_incl", [P, NG, B, P])
        decay_strict = sb("decay_strict", [P, NG, B, P])
        LT = sb("LT", [P, NG, B, P])
        AT = sb("AT", [P, NG, B, P])
        TT = sb("TT", [P, NG, B, P])
        TN = sb("TN", [P, NG, B, P])
        joined = sb("joined", [P, NG, B, P])
        u = sb("u", [P, NG, B, D])
        state = sb("state", [P, B, D])
        seen = sb("seen", [P, 2, B, 2, D])
        resid = sb("resid", [P, 2, B, D])
        o_tok = sb("o_tok", [P, NT, P])
        o_square = sb("o_square", [P, NT, P])
        o_sum = sb("o_sum", [P, 2 * NT])
        o_sum_e = sb("o_sum_e", [P, 2 * NT])
        o_rnorm = sb("o_rnorm", [P, 2 * NT])
        o_unit = sb("o_unit", [P, NT, P])
        o_out = sb("o_out", [P, NT, P])
        oT = sb("oT", [P, B * T])

        pads_zero = sem("pads_zero")
        proj_done = sem("proj_done")
        pad_done = sem("pad_done")
        z_in_psum = sem("z_in_psum")
        z_tanh_done = sem("z_tanh_done")
        w_gated_done = sem("w_gated_done")
        conv_step = sem("conv_step")
        tok_in_psum = sem("tok_in_psum")
        square_done = sem("square_done")
        ssum_done = sem("ssum_done")
        ssum_e_done = sem("ssum_e_done")
        rnorm_done = sem("rnorm_done")
        qk_tok_done = sem("qk_tok_done")
        v_tok_done = sem("v_tok_done")
        k_rest_done = sem("k_rest_done")
        qkT_in_psum = sem("qkT_in_psum")
        qkT_done = sem("qkT_done")
        g_tri_done = sem("g_tri_done")
        decay_in_psum = sem("decay_in_psum")
        decay_done = sem("decay_done")
        masked_done = sem("masked_done")
        kk_in_psum = sem("kk_in_psum")
        LT_done = sem("LT_done")
        AT_done = sem("AT_done")
        pairs_done = sem("pairs_done")
        TT_done = sem("TT_done")
        TN_in_psum = sem("TN_in_psum")
        TN_done = sem("TN_done")
        join_in_psum = sem("join_in_psum")
        joined_done = sem("joined_done")
        delta_in_psum = sem("delta_in_psum")
        u_in_psum = sem("u_in_psum")
        u_done = sem("u_done")
        state_in_psum = sem("state_in_psum")
        state_done = sem("state_done")
        seen_in_psum = sem("seen_in_psum")
        seen_done = sem("seen_done")
        resid_done = sem("resid_done")
        o_in_psum = sem("o_in_psum")
        o_tok_done = sem("o_tok_done")
        o_square_done = sem("o_square_done")
        o_sum_done = sem("o_sum_done")
        o_sum_e_done = sem("o_sum_e_done")
        o_rnorm_done = sem("o_rnorm_done")
        o_unit_done = sem("o_unit_done")
        o_out_done = sem("o_out_done")
        oT_in_psum = sem("oT_in_psum")
        oT_done = sem("oT_done")
        y_in_psum = sem("y_in_psum")
        x_done = sem("x_done")

        def four(bank):
            return PS[:, bank, :].rearrange("p (b t) -> p b t", b=4)

        G = [four(4 + q) for q in range(NG)]
        with nc.Block() as block:

            @block.sync
            def _(sp):
                sp.dma_start(w_pair[:, :].unsqueeze(1), w_src(0)).then_inc(w_loaded, 16)
                sp.dma_start(w_out[:, :].unsqueeze(1), wo_src(0)).then_inc(wo_loaded, 16)
                with sp.Fori(1, NP) as p:
                    pair = sp.snap(p)
                    sp.wait_ge(qk_tok_done, pair * 4)
                    sp.dma_start(w_pair[:, :].unsqueeze(1), w_src(pair)).then_inc(w_loaded, 16)
                    sp.wait_ge(w_gated_done, pair)
                    sp.dma_start(w_out[:, :].unsqueeze(1), wo_src(pair)).then_inc(wo_loaded, 16)

            @block.tensor
            def _(pe):
                def project(p):
                    pe.wait_ge(w_loaded, p * 16 + 16)
                    for m in range(6):
                        j, half = m // 2, m % 2
                        if m >= 2:
                            pe.wait_ge(pad_done, p * 6 + m - 1)
                        for c in range(KC):
                            w0 = (c * 4 + j) * P
                            last = pe.matmul(PS[:, m % 2, :], w_pair[:, w0:w0 + P],
                                             xT[:, c, half * 512:(half + 1) * 512],
                                             start=(c == 0), stop=(c == KC - 1))
                        last.then_inc(proj_done, 1)
                    for n in range(NT):
                        for c in range(KC):
                            w0 = (c * 4 + 3) * P
                            last = pe.matmul(PS[:, 2 + n // 4, n % 4 * P:(n % 4 + 1) * P],
                                             xT[:, c, n * P:(n + 1) * P], w_pair[:, w0:w0 + P],
                                             start=(c == 0), stop=(c == KC - 1))
                        if n % 4 == 3:
                            last.then_inc(z_in_psum, 1)

                def to_tokens(p, m):
                    j, half = m // 2, m % 2
                    pe.wait_ge(conv_step, p * 12 + 4 * (j + 1))
                    if m == 0:
                        pe.wait_ge(z_tanh_done, p * 2 + 1)
                    if m == 1:
                        pe.wait_ge(z_tanh_done, p * 2 + 2)
                    if 2 <= m <= 5:
                        pe.wait_ge(qk_tok_done, p * 4 + m - 1)
                    flat = conv[:, j, :, :].rearrange("p b t -> p (b t)")
                    for n in range(4):
                        t0 = (4 * half + n) * P
                        last = pe.transpose(PS[:, 2 + m % 2, n * P:(n + 1) * P], flat[:, t0:t0 + P], ident[:, :])
                    last.then_inc(tok_in_psum, 1)

                def to_channels(p, m):
                    pe.wait_ge(qk_tok_done, p * 4 + m + 1)
                    if m < 2:
                        pe.wait_ge(pad_done, p * 6 + 5 + m)
                    else:
                        pe.wait_ge(qkT_done, p * 4 + m - 1)
                    for n in range(4):
                        last = pe.transpose(PS[:, m % 2, n * P:(n + 1) * P],
                                            qk_tok[:, m // 2, 4 * (m % 2) + n, :], ident[:, :])
                    last.then_inc(qkT_in_psum, 1)

                with pe.Fori(0, NP) as p:
                    project(p)
                    for m in range(6):
                        to_tokens(p, m)
                    for m in range(4):
                        to_channels(p, m)
                    for q in range(NG):
                        pe.wait_ge(g_tri_done, p * NG + q + 1)
                        pe.matmul(PS[:, 4 + q, :], after[:, :], g_tri[:, q % 2, :, :].rearrange("p b t -> p (b t)"),
                                  start=True, stop=True).then_inc(decay_in_psum, 1)
                    pe.wait_ge(qkT_done, p * 4 + 4)
                    for m in range(2 * NG):
                        q, pairb = m // 2, m % 2
                        hd, ch = q // 2, q % 2
                        if m < 4:
                            pe.wait_ge(decay_done, p * NG + m + 1)
                        else:
                            pe.wait_ge(AT_done, p * 2 * NG + m - 3)
                        for e in range(2):
                            n = 2 * (2 * pairb + e) + ch
                            rows = qkT[hd * D:(hd + 1) * D, n, :, :]
                            last = pe.matmul(PS[:, 4 + m % 4, e * 2 * P:(e + 1) * 2 * P], rows[:, 0, :],
                                             rows.rearrange("p a t -> p (a t)"), start=True, stop=True)
                        last.then_inc(kk_in_psum, 1)
                    pe.wait_ge(AT_done, (p + 1) * 2 * NG)

                    def turn(lv, q):
                        if lv == 0:
                            pe.wait_ge(pairs_done, p * 2 * NG + 2 * q + 2)
                        else:
                            pe.wait_ge(TT_done, p * NL * NG + (lv - 1) * NG + q + 1)
                        for b in range(B):
                            last = pe.transpose(G[q][:, b, :], TT[:, q, b, :], ident[:, :])
                        last.then_inc(TN_in_psum, 1)

                    for q in range(NG):
                        turn(0, q)
                    for lv in range(NL):
                        for q in range(NG):
                            pe.wait_ge(TN_done, (p * NL + lv) * NG + q + 1)
                            for b in range(B):
                                last = pe.matmul(G[q][:, b, :], LT[:, q, b, :], TN[:, q, b, :],
                                                 start=True, stop=True)
                            last.then_inc(join_in_psum, 1)
                        for q in range(NG):
                            pe.wait_ge(joined_done, (p * NL + lv) * NG + q + 1)
                            for b in range(B):
                                last = pe.matmul(G[q][:, b, :], joined[:, q, b, :], TT[:, q, b, :],
                                                 start=True, stop=True)
                            last.then_inc(delta_in_psum, 1)
                        if lv < NL - 1:
                            for q in range(NG):
                                turn(lv + 1, q)
                    for hd in range(2):
                        q = 2 * hd
                        pe.wait_ge(TT_done, p * NL * NG + (NL - 1) * NG + q + 1)
                        pe.wait_ge(v_tok_done, p * 2 + 2)
                        for b in range(B):
                            last = pe.matmul(G[q][:, b, 0:D], TT[:, q, b, :], v_tok[:, 2 * b, hd * D:(hd + 1) * D],
                                             start=True, stop=True)
                        last.then_inc(u_in_psum, 1)
                    for hd in range(2):
                        q = 2 * hd
                        pe.wait_ge(u_done, p * NG + hd + 1)
                        pe.wait_ge(k_rest_done, p + 1)
                        pe.wait_ge(TT_done, p * NL * NG + (NL - 1) * NG + q + 2)
                        for b in range(B):
                            last = pe.matmul(G[q + 1][hd * D:(hd + 1) * D, b, 0:D],
                                             k_rest[:, b, hd * D:(hd + 1) * D], u[:, q, b, :],
                                             start=True, stop=True)
                        last.then_inc(state_in_psum, 1)
                        for b in range(B):
                            last = pe.matmul(G[q][:, b, 0:D], AT[:, q, b, :], u[:, q, b, :],
                                             start=True, stop=True)
                        last.then_inc(o_in_psum, 1)
                    for hd in range(2):
                        q = 2 * hd + 1
                        pe.wait_ge(state_done, p * 2 + hd + 1)
                        for b in range(B):
                            for a in range(2):
                                rows = slice(hd * D, (hd + 1) * D)
                                last = pe.matmul(G[q][:, b, a * D:(a + 1) * D], qkT[rows, 2 * b + 1, a, :],
                                                 state[rows, b, :], start=True, stop=True)
                        last.then_inc(seen_in_psum, 1)
                    for hd in range(2):
                        q = 2 * hd + 1
                        pe.wait_ge(resid_done, p * 2 + hd + 1)
                        for b in range(B):
                            last = pe.matmul(G[q][:, b, 0:D], TT[:, q, b, :], resid[:, hd, b, :],
                                             start=True, stop=True)
                        last.then_inc(u_in_psum, 1)
                    for hd in range(2):
                        q = 2 * hd + 1
                        pe.wait_ge(u_done, p * NG + 2 + hd + 1)
                        for b in range(B):
                            last = pe.matmul(G[q][:, b, 0:D], AT[:, q, b, :], u[:, q, b, :],
                                             start=True, stop=True)
                        last.then_inc(o_in_psum, 1)
                    pe.wait_ge(o_out_done, p * 2 + 2)
                    for n in range(NT):
                        last = pe.transpose(PS[:, 4 + n // 4, n % 4 * P:(n % 4 + 1) * P], o_out[:, n, :], ident[:, :])
                        if n % 4 == 3:
                            last.then_inc(oT_in_psum, 1)
                    pe.wait_ge(w_gated_done, p + 1)
                    pe.wait_ge(oT_done, p * 2 + 2)
                    for n in range(NT):
                        last = pe.matmul(PS[:, 4 + n // 2, n % 2 * H:(n % 2 + 1) * H], oT[:, n * P:(n + 1) * P],
                                         w_gated[:, :], start=True, stop=True)
                        if n % 2:
                            last.then_inc(y_in_psum, 1)
                    pe.wait_ge(x_done, p * 4 + 4)

            @block.scalar
            def _(act):
                act.wait_ge(pads_zero, 1)
                with act.Fori(0, NP) as p:
                    for m in range(6):
                        j, half = m // 2, m % 2
                        act.wait_ge(proj_done, p * 6 + m + 1)
                        nc.scalar.copy(pad[:, j, 2 * half:2 * half + 2, TAPS - 1:PADT],
                                       PS[:, m % 2, :].rearrange("p (b t) -> p b t", b=2)).then_inc(pad_done, 1)
                    for m in range(2):
                        act.wait_ge(z_in_psum, p * 2 + m + 1)
                        nc.scalar.activation(z_tanh[:, 4 * m:4 * m + 4, :], four(2 + m), ACT.Tanh, scale=0.5)\
                            .then_inc(z_tanh_done, 1)
                    for m in range(4):
                        act.wait_ge(tok_in_psum, p * 6 + m + 1)
                        if m >= 2:
                            act.wait_ge(ssum_done, p * 4 + m - 1)
                        nc.scalar.activation(square[:, m % 2], four(2 + m % 2), ACT.Square,
                                             scale=float(D) ** 0.5 if m < 2 else 1.0).then_inc(square_done, 1)
                    for m in range(2):
                        act.wait_ge(tok_in_psum, p * 6 + 5 + m)
                        nc.scalar.copy(v_tok[:, 4 * m:4 * m + 4, :], four(2 + m)).then_inc(v_tok_done, 1)
                    for m in range(4):
                        act.wait_ge(qkT_in_psum, p * 4 + m + 1)
                        nc.scalar.copy(qkT[:, 4 * (m % 2):4 * (m % 2) + 4, 1 - m // 2, :], four(m % 2))\
                            .then_inc(qkT_done, 1)
                    for q in range(NG):
                        act.wait_ge(decay_in_psum, p * NG + q + 1)
                        if q >= 2:
                            act.wait_ge(masked_done, p * 2 * NG + 2 * (q - 1))
                        nc.scalar.activation(decay[:, q % 2], G[q], ACT.Exp).then_inc(decay_done, 1)
                    for lv in range(NL):
                        for q in range(NG):
                            act.wait_ge(TN_in_psum, (p * NL + lv) * NG + q + 1)
                            nc.scalar.copy(TN[:, q], G[q]).then_inc(TN_done, 1)
                    for hd in range(2):
                        rows = slice(hd * D, (hd + 1) * D)
                        act.wait_ge(state_in_psum, p * 2 + hd + 1)
                        nc.scalar.copy(state[rows, :, :], G[2 * hd + 1][rows, :, 0:D]).then_inc(state_done, 1)
                    act.wait_ge(wo_loaded, p * 16 + 16)
                    nc.scalar.activation(w_gated[:, :], w_out[:, :], ACT.Copy, scale=gate_w[:, 0:1])\
                        .then_inc(w_gated_done, 1)
                    act.wait_ge(o_tok_done, p * NG + NG)
                    nc.scalar.activation(o_square[:, :, :], o_tok[:, :, :], ACT.Square,
                                         scale=float(D) ** -0.5).then_inc(o_square_done, 1)
                    for m in range(2):
                        act.wait_ge(oT_in_psum, p * 2 + m + 1)
                        nc.scalar.copy(oT[:, 512 * m:512 * (m + 1)], PS[:, 4 + m, :]).then_inc(oT_done, 1)

            @block.vector
            def _(dve):
                with dve.Fori(0, NP) as p:
                    for j in range(3):
                        dve.wait_ge(pad_done, p * 6 + 2 * j + 2)
                        for tap in range(TAPS - 1, -1, -1):
                            w0 = KC * 4 * P + j * TAPS + tap
                            src = pad[:, j, :, tap:tap + T]
                            if tap == TAPS - 1:
                                last = nc.vector.tensor_scalar(conv[:, j], src, w_pair[:, w0:w0 + 1], None, ALU.mult)
                            else:
                                dve.wait_ge(conv_step, p * 12 + j * TAPS + TAPS - 1 - tap)
                                last = nc.vector.scalar_tensor_tensor(
                                    out=conv[:, j], in0=src, scalar=w_pair[:, w0:w0 + 1], in1=conv[:, j],
                                    op0=ALU.mult, op1=ALU.add)
                            last.then_inc(conv_step, 1)
                    for m in range(4):
                        dve.wait_ge(square_done, p * 4 + m + 1)
                        nc.vector.tensor_reduce(ssum[:, m, :], square[:, m % 2].rearrange("p n (h d) -> p (n h) d", h=2),
                                                AX.X, ALU.add).then_inc(ssum_done, 1)
                        dve.wait_ge(rnorm_done, p * 4 + m + 1)
                        nc.vector.tensor_tensor(
                            qk_tok[:, m // 2, 4 * (m % 2):4 * (m % 2) + 4, :].rearrange("p n (h d) -> p (n h) d", h=2),
                            PS[:, 2 + m % 2, :].rearrange("p (a d) -> p a d", d=D), bc(rnorm[:, m, :], 2, D),
                            ALU.mult).then_inc(qk_tok_done, 1)
                    for m in range(2 * NG):
                        q, pairb = m // 2, m % 2
                        hd, ch = q // 2, q % 2
                        dve.wait_ge(kk_in_psum, p * 2 * NG + m + 1)
                        dve.wait_ge(masked_done, p * 2 * NG + 2 * q + 2)
                        prod = PS[:, 4 + m % 4, :].rearrange("p (e a t) -> p e a t", e=2, a=2)
                        for e in range(2):
                            b = 2 * pairb + e
                            bt = beta[:, bass.ds(2 * p + hd, 1), 2 * b + ch]
                            nc.vector.scalar_tensor_tensor(out=LT[:, q, b, :], in0=prod[:, e, 0, :], scalar=bt,
                                                           in1=decay_strict[:, q, b, :], op0=ALU.mult,
                                                           op1=ALU.mult).then_inc(LT_done, 1)
                        nc.vector.tensor_tensor(AT[:, q, 2 * pairb:2 * pairb + 2, :], prod[:, :, 1, :],
                                                decay_incl[:, q, 2 * pairb:2 * pairb + 2, :], ALU.mult)\
                            .then_inc(AT_done, 1)
                    for lv in range(NL):
                        for q in range(NG):
                            dve.wait_ge(join_in_psum, (p * NL + lv) * NG + q + 1)
                            nc.vector.tensor_tensor(joined[:, q], G[q], bc(off_mask[:, lv, :], 1, B), ALU.mult)\
                                .then_inc(joined_done, 1)
                        for q in range(NG):
                            dve.wait_ge(delta_in_psum, (p * NL + lv) * NG + q + 1)
                            nc.vector.tensor_tensor(TT[:, q], TT[:, q], G[q], ALU.subtract).then_inc(TT_done, 1)

                    def by_head(t, hd, ch):
                        return bc(t[:, bass.ds(2 * p + hd, 1), ch:NT:2].rearrange("p o n -> p (o n)"), 2, D)

                    for hd in range(2):
                        dve.wait_ge(u_in_psum, p * NG + hd + 1)
                        nc.vector.tensor_tensor(u[:, 2 * hd], G[2 * hd][:, :, 0:D], by_head(beta, hd, 0), ALU.mult)\
                            .then_inc(u_done, 1)
                    for hd in range(2):
                        dve.wait_ge(o_in_psum, p * NG + hd + 1)
                        nc.vector.tensor_copy(o_tok[:, 0:NT:2, hd * D:(hd + 1) * D], G[2 * hd][:, :, 0:D])\
                            .then_inc(o_tok_done, 1)
                    for hd in range(2):
                        dve.wait_ge(seen_in_psum, p * 2 + hd + 1)
                        ds_ = bass.ds(2 * p + hd, 1)
                        dec = bc(grow[:, ds_, 1:NT:2].rearrange("p o n -> p (o n)"), 2, 2 * D)
                        nc.vector.tensor_tensor(seen[:, hd].rearrange("p b a d -> p b (a d)"), G[2 * hd + 1],
                                                dec, ALU.mult).then_inc(seen_done, 1)
                        dve.wait_ge(seen_done, p * 2 + hd + 1)
                        nc.vector.tensor_tensor(resid[:, hd], v_tok[:, 1:NT:2, hd * D:(hd + 1) * D],
                                                seen[:, hd, :, 0, :], ALU.subtract).then_inc(resid_done, 1)
                    for hd in range(2):
                        dve.wait_ge(u_in_psum, p * NG + 2 + hd + 1)
                        nc.vector.tensor_tensor(u[:, 2 * hd + 1], G[2 * hd + 1][:, :, 0:D], by_head(beta, hd, 1),
                                                ALU.mult).then_inc(u_done, 1)
                    for hd in range(2):
                        dve.wait_ge(o_in_psum, p * NG + 2 + hd + 1)
                        nc.vector.tensor_tensor(o_tok[:, 1:NT:2, hd * D:(hd + 1) * D], G[2 * hd + 1][:, :, 0:D],
                                                seen[:, hd, :, 1, :], ALU.add).then_inc(o_tok_done, 1)
                    dve.wait_ge(o_square_done, p + 1)
                    nc.vector.tensor_reduce(o_sum[:, :], o_square[:, :, :].rearrange("p n (h d) -> p (n h) d", h=2),
                                            AX.X, ALU.add).then_inc(o_sum_done, 1)
                    dve.wait_ge(o_rnorm_done, p + 1)
                    nc.vector.tensor_tensor(o_unit[:, :, :].rearrange("p n (h d) -> p (n h) d", h=2),
                                            o_tok[:, :, :].rearrange("p n (h d) -> p (n h) d", h=2),
                                            bc(o_rnorm[:, :], 2, D), ALU.mult).then_inc(o_unit_done, 1)
                    dve.wait_ge(o_unit_done, p + 1)
                    for m in range(2):
                        nc.vector.scalar_tensor_tensor(out=o_out[:, 4 * m:4 * m + 4, :],
                                                       in0=z_tanh[:, 4 * m:4 * m + 4, :], scalar=1.0,
                                                       in1=o_unit[:, 4 * m:4 * m + 4, :], op0=ALU.add,
                                                       op1=ALU.mult).then_inc(o_out_done, 1)
                    for m in range(4):
                        dve.wait_ge(y_in_psum, p * 4 + m + 1)
                        xs = X[:, 2 * m:2 * m + 2, :]
                        nc.vector.tensor_tensor(xs, xs, PS[:, 4 + m, :].rearrange("p (n d) -> p n d", n=2), ALU.add)\
                            .then_inc(x_done, 1)

            @block.gpsimd
            def _(pool):
                pool.memset(pad[:, :, :, :], 0.0).then_inc(pads_zero, 1)
                with pool.Fori(0, NP) as p:
                    def make_g_tri(q):
                        hd, ch = q // 2, q % 2
                        if q >= 2:
                            pool.wait_ge(decay_in_psum, p * NG + q - 1)
                        col = g[:, bass.ds(2 * p + hd, 1), ch:NT:2].rearrange("p o n -> p (o n)")
                        pool.tensor_tensor(g_tri[:, q % 2], bc(k.tri_incl[:, :], 1, B), bc(col, 2, P), ALU.mult)\
                            .then_inc(g_tri_done, 1)

                    make_g_tri(0)
                    make_g_tri(1)
                    for m in range(4):
                        pool.wait_ge(ssum_done, p * 4 + m + 1)
                        pool.tensor_tensor(ssum_e[:, m, :], ssum[:, m, :], norm_eps[:, 8 * (m // 2):8 * (m // 2) + 8],
                                           ALU.add).then_inc(ssum_e_done, 1)
                        pool.wait_ge(ssum_e_done, p * 4 + m + 1)
                        pool.tensor_tensor(rnorm[:, m, :], ssum_e[:, m, :], neg_half[:, 0:8], ALU.pow)\
                            .then_inc(rnorm_done, 1)
                    pool.wait_ge(qk_tok_done, p * 4 + 4)
                    for hd in range(2):
                        ds_ = bass.ds(2 * p + hd, 1)
                        col = rest[:, ds_, 0:NT:2].rearrange("p o n -> p (o n)")
                        last = pool.tensor_tensor(k_rest[:, :, hd * D:(hd + 1) * D],
                                                  qk_tok[:, 1, 0:NT:2, hd * D:(hd + 1) * D], bc(col, 2, D), ALU.mult)
                    last.then_inc(k_rest_done, 1)
                    for q in range(NG):
                        if q >= 2:
                            make_g_tri(q)
                        pool.wait_ge(decay_done, p * NG + q + 1)
                        pool.tensor_tensor(decay_incl[:, q], decay[:, q % 2], bc(k.tri_incl[:, :], 1, B), ALU.mult)\
                            .then_inc(masked_done, 1)
                        pool.affine_select(out=decay_strict[:, q], in_=decay[:, q % 2], compare_op=ALU.is_gt, fill=0.0,
                                           base=0, pattern=[[0, B], [1, P]], channel_multiplier=-1)\
                            .then_inc(masked_done, 1)
                    for q in range(NG):
                        pool.wait_ge(LT_done, (p * NG + q) * B + B)
                        pool.tensor_tensor(TT[:, q], LT[:, q], bc(pair_mask[:, :], 1, B), ALU.mult)\
                            .then_inc(pairs_done, 1)
                        pool.wait_ge(pairs_done, p * 2 * NG + 2 * q + 1)
                        pool.tensor_tensor(TT[:, q], bc(ident[:, :], 1, B), TT[:, q], ALU.subtract)\
                            .then_inc(pairs_done, 1)
                    pool.wait_ge(o_sum_done, p + 1)
                    pool.tensor_tensor(o_sum_e[:, :], o_sum[:, :], o_eps[:, :], ALU.add)\
                        .then_inc(o_sum_e_done, 1)
                    pool.wait_ge(o_sum_e_done, p + 1)
                    pool.tensor_tensor(o_rnorm[:, :], o_sum_e[:, :], neg_half[:, :], ALU.pow)\
                        .then_inc(o_rnorm_done, 1)


def build(nc, I_, out):
    k = Core()
    k.nc = nc
    k.bufs = [nc.dram_tensor(f"slot_rows{run}", [E * CAP, H], F32).ap() for run in range(2)]
    results = [nc.dram_tensor(f"slot_results{run}", [E * CAP, H], F32).ap() for run in range(2)]
    with ExitStack() as ctx:
        def sb(name, shape):
            return ctx.enter_context(nc.sbuf_tensor(name, shape, F32))

        k.X = sb("residual", [P, NT, H])
        k.ident = sb("ident", [P, P])
        k.tri_incl = sb("tri_incl", [P, P])
        k.tri_strict = sb("tri_strict", [P, P])
        k.eps = sb("ln_eps", [P, 1])
        k.PS = ctx.enter_context(nc.psum_tensor("psum", [P, 8, 512], F32))
        stage_load(k, I_)
        stage_attention_a(k, I_)
        stage_moe(k, I_, 0, k.bufs[0], results[0])
        stage_delta(k, I_)
        stage_moe(k, I_, 1, k.bufs[1], results[1])
        with semaphores(nc) as take, nc.Block() as block:
            stored = take("stored_out")

            @block.sync
            def _(sp):
                sp.dma_start(out.rearrange("b (h p) d -> p (b h) d", p=P), k.X[:, :, :]).then_inc(stored, 16)
                sp.wait_ge(stored, 16)


def host_constants():
    f = np.float32
    lower = np.tril(np.ones((P, P), f))
    inv = (f(1.0) / f(10000.0) ** (np.arange(0, HSA, 2, dtype=f) / f(HSA))).astype(f)
    ang = np.arange(T, dtype=f)[:, None] * inv[None, :]
    c, s = np.cos(ang).astype(f), np.sin(ang).astype(f)
    cos = np.concatenate([c, c], 1).reshape(2, P, HSA)
    sin = np.concatenate([-s, s], 1).reshape(2, P, HSA)
    scale = np.array([HSA ** -0.5, 1.0], f)
    out = {
        "ident": np.eye(P, dtype=f),
        "tri_incl": np.ascontiguousarray(lower.T),
        "tri_strict": np.ascontiguousarray(np.triu(np.ones((P, P), f), 1)),
        "a_cos": np.ascontiguousarray((cos[:, :, None, :] * scale[None, None, :, None]).transpose(1, 0, 2, 3)),
        "a_sin": np.ascontiguousarray((sin[:, :, None, :] * scale[None, None, :, None]).transpose(1, 0, 2, 3)),
        "a_head_rows": np.repeat(np.eye(HPT, dtype=f), HSA, 0),
    }
    out["m_expert_no"] = np.tile(np.arange(E, dtype=f), (P, 1))
    out["zeros"] = np.zeros((P, E * CAP * H // P), f)
    out["after"] = np.ascontiguousarray(np.tril(np.ones((P, P), f), -1))
    i, j = np.arange(P)[:, None], np.arange(P)[None, :]
    out["off_mask"] = np.ascontiguousarray(np.stack(
        [((i // s) % 2 == 1) & (j // s == i // s - 1) for s in LEVELS], 1).astype(f))
    out["pair_mask"] = ((j % 2 == 1) & (i == j - 1)).astype(f)
    return out


def lay_out(x):
    c = np.ascontiguousarray
    g = {n: np.asarray(a) for n, a in x.items()}
    a = "L0_attn_a_"
    even_odd = np.arange(H).reshape(NHA, HSA // 2, 2).transpose(0, 2, 1).ravel()
    w = np.concatenate([g[a + "Wq"][:, even_odd], g[a + "Wk"][:, even_odd], g[a + "Wv"]], 1)
    out = {
        "x": c(g[a + "x"]),
        "a_w_qkv": c(w.reshape(KC, P, 3 * H).transpose(1, 0, 2)),
        "a_b_qkv": c(np.concatenate([g[a + "bq"][even_odd], g[a + "bk"][even_odd], g[a + "bv"]])),
        "a_w_o": c(g[a + "Wo"].reshape(KC, P, H).transpose(1, 0, 2)),
        "a_b_o": c(g[a + "bo"]),
    }
    m = "L0_ffn_"
    gu = np.concatenate([g[m + "w_gate"], g[m + "w_up"]], 2)
    down = np.zeros((len(SHC) * P, H), np.float32)
    down[:IS] = g[m + "ws_down"]
    out.update({
        "m_w_router": c(g[m + "gate_w"].T.reshape(KC, P, E).transpose(1, 0, 2)),
        "m_w_gu": c(gu.reshape(E, KC, P, 2 * I).transpose(0, 2, 1, 3).reshape(E, P, KC * 2 * I)),
        "m_w_d": c(g[m + "w_down"].reshape(E, 2, IH, H).transpose(0, 2, 1, 3).reshape(E, IH, 2 * H)),
        "m_w_sg": c(g[m + "ws_gate"].reshape(KC, P, IS).transpose(1, 0, 2)),
        "m_w_su": c(g[m + "ws_up"].reshape(KC, P, IS).transpose(1, 0, 2)),
        "m_w_sd": c(down.reshape(len(SHC), P, H).transpose(1, 0, 2)),
    })
    d = "L0_attn_b_"
    wt = g[d + "w_qkvz"].reshape(NP, 2, 4, D, KC, P).transpose(0, 5, 4, 2, 1, 3).reshape(NP, P, KC * 4 * P)
    taps = g[d + "conv_w"].reshape(3, NP, P, TAPS).transpose(1, 2, 0, 3).reshape(NP, P, 3 * TAPS)
    ba = g[d + "w_ba"].reshape(NH, 2, KC, P).transpose(3, 2, 1, 0).reshape(P, KC, 2 * NH)
    out.update({
        "d_w_pair": c(np.concatenate([wt, taps], 2)),
        "d_w_ba": c(ba),
        "d_w_out": c(g[d + "w_out"].T.reshape(NP, P, H)),
        "d_a_log": c(g[d + "A_log"]),
        "d_dt_bias": c(g[d + "dt_bias"]),
        "d_norm_w": c(np.concatenate([g[d + "norm_weight"]] * 2)[:, None]),
    })
    return out


def kernel(**inputs):
    import concourse.bacc as _bacc
    from concourse.bass_utils import run_bass_kernel_spmd as _run

    nc = _bacc.Bacc("TRN2", target_bir_lowering=False, num_devices=1)
    arrays = {**host_constants(), **lay_out(inputs)}
    I_ = {n: nc.dram_tensor("in_" + n, a.shape, mybir.dt.from_np(a.dtype), kind="ExternalInput").ap()
          for n, a in arrays.items()}
    out = nc.dram_tensor("out_x", [B, T, H], F32, kind="ExternalOutput").ap()
    build(nc, I_, out)
    r = _run(nc, [{"in_" + n: a for n, a in arrays.items()}], core_ids=[0])
    return r.results[0]["out_x"]
```

```python
import numpy as np

import concourse.bass as bass
from concourse import mybir
from contextlib import ExitStack, contextmanager

F32 = mybir.dt.float32
BF16 = mybir.dt.bfloat16
U32 = mybir.dt.uint32
ALU = mybir.AluOpType
ACT = mybir.ActivationFunctionType
AX = mybir.AxisListType

P = 128
B, T, H = 4, 256, 256
NT = B * T // P
KC = H // P
LN_EPS = 1e-5

NHA, HSA = 16, 16
HPT = P // HSA
VPITCH = P + HSA

E, I, CAP = 16, 176, 128
IS = 2 * I
IH = I // 2
SHC = [(0, 128), (128, 128), (256, 96)]

NH, D = 32, 64
NP = NH // 2
TAPS = 4
PADT = T + TAPS - 1
GEPS = 1e-6


class Core:
    pass


def bc(ap, axis, n):
    v = ap.unsqueeze(axis)
    return v.to_broadcast([n if a == axis else s for a, s in enumerate(v.shape)])


@contextmanager
def semaphores(nc):
    taken = []

    def take(name):
        taken.append(nc.alloc_semaphore(name=name))
        return taken[-1]

    yield take
    nc.all_engine_barrier()
    nc.clear_and_free_semaphores(taken)
    nc.all_engine_barrier()


def stage_load(k, I_):
    nc = k.nc
    with semaphores(nc) as take, nc.Block() as block:
        loaded = take("common_loaded")

        @block.sync
        def _(sp):
            xs = I_["x"].rearrange("b (h p) d -> p (b h) d", p=P)
            sp.dma_start(k.X[:, :, :], xs).then_inc(loaded, 16)
            for dst, src in ((k.ident, "ident"), (k.tri_incl, "tri_incl"), (k.tri_strict, "tri_strict")):
                sp.dma_start(dst[:, :], I_[src]).then_inc(loaded, 16)
            sp.wait_ge(loaded, 4 * 16)

        @block.gpsimd
        def _(pool):
            pool.memset(k.eps[:, :], LN_EPS)


def stage_attention_a(k, I_):
    nc, X, ident, PS = k.nc, k.X, k.ident, k.PS
    NS = NHA
    with semaphores(nc) as take, ExitStack() as ctx:
        def sb(name, shape, dt=F32):
            return ctx.enter_context(nc.sbuf_tensor(name, shape, dt))

        def sem(name):
            return take(name)

        w_qkv = sb("a_w_qkv", [P, KC, 3 * H])
        b_qkv = sb("a_b_qkv", [P, 3 * H])
        w_o = sb("a_w_o", [P, KC, H])
        b_o = sb("a_b_o", [P, H])
        cos = sb("a_cos", [P, 2, 2, HSA])
        sin = sb("a_sin", [P, 2, 2, HSA])
        head_rows = sb("a_head_rows", [P, HPT])
        stats = sb("a_stats", [P, NT, 6])
        mv = sb("a_mv", [P, NT, 2])
        std = sb("a_std", [P, NT])
        rstd = sb("a_rstd", [P, NT])
        xn = sb("a_xn", [P, 2, H])
        xT = sb("a_xT", [P, KC, T])
        qk = sb("a_qk", [P, 2, 2 * H])
        qk_cos = sb("a_qk_cos", [P, 2, 2 * H])
        qk_sin = sb("a_qk_sin", [P, 2, 2 * H])
        qT = sb("a_qT", [P, 2, 2, T])
        kT = sb("a_kT", [P, 2, 2, HPT, T])
        v_pad = sb("a_v_pad", [P, 2, 2, 2, HPT * VPITCH])
        neg_max = sb("a_neg_max", [P, 4, 2])
        row_sum = sb("a_row_sum", [P, 4, 2])
        row_inv = sb("a_row_inv", [P, 4, 2])
        probs = sb("a_probs", [P, 3, 2, T])
        probsT = sb("a_probsT", [P, 2, 2, 2, T])
        oT = sb("a_oT", [P, 2, T])
        y = sb("a_y", [P, 2, H])

        loaded = sem("a_loaded")
        slots_zero = sem("a_slots_zero")
        v_zero = sem("a_v_zero")
        stats_done = sem("a_stats_done")
        mv_done = sem("a_mv_done")
        std_done = sem("a_std_done")
        rstd_done = sem("a_rstd_done")
        xn_done = sem("a_xn_done")
        xT_in_psum = sem("a_xT_in_psum")
        xT_done = sem("a_xT_done")
        qkv_in_psum = sem("a_qkv_in_psum")
        qk_done = sem("a_qk_done")
        rope_parts = sem("a_rope_parts")
        rope_done = sem("a_rope_done")
        qkT_in_psum = sem("a_qkT_in_psum")
        qT_done = sem("a_qT_done")
        kT_done = sem("a_kT_done")
        scores_done = sem("a_scores_done")
        max_done = sem("a_max_done")
        exp_done = sem("a_exp_done")
        inv_done = sem("a_inv_done")
        probs_done = sem("a_probs_done")
        probsT_in_psum = sem("a_probsT_in_psum")
        diag_done = sem("a_diag_done")
        full_done = sem("a_full_done")
        av_done = sem("a_av_done")
        oT_done = sem("a_oT_done")
        y_in_psum = sem("a_y_in_psum")
        y_done = sem("a_y_done")
        x_done = sem("a_x_done")

        SC = [PS[:, j, :].rearrange("p (h t) -> p h t", h=2) for j in range(3)]
        TR = [PS[:, 3 + j, :].rearrange("p (h c t) -> p h c t", h=2, c=2) for j in range(2)]
        OT = [PS[:, 5, 0:T], PS[:, 6, 0:T]]
        BANK = PS[:, 7, :]
        QKT = BANK.rearrange("p (u n t) -> p u n t", u=2, n=2)
        YB = BANK.rearrange("p (n d) -> p n d", n=2)

        def first(i):
            return isinstance(i, int) and i == 0

        with nc.Block() as block:

            @block.sync
            def _(sp):
                for dst, name in ((w_qkv, "a_w_qkv"), (w_o, "a_w_o"), (cos, "a_cos"), (sin, "a_sin"),
                                  (head_rows, "a_head_rows")):
                    sp.dma_start(dst[tuple(slice(None) for _ in dst.shape)], I_[name]).then_inc(loaded, 16)
                sp.dma_start(b_qkv[:, :], I_["a_b_qkv"].partition_broadcast(P)).then_inc(loaded, 16)
                sp.dma_start(b_o[:, :], I_["a_b_o"].partition_broadcast(P)).then_inc(loaded, 16)
                sp.wait_ge(loaded, 7 * 16)
                for bufs in k.bufs:
                    sp.dma_start(bufs.rearrange("(p r) d -> p (r d)", p=P), I_["zeros"]).then_inc(slots_zero, 16)
                sp.wait_ge(slots_zero, 16 * len(k.bufs))

            @block.gpsimd
            def _(pool):
                pool.memset(v_pad[:, :, :, :, :], 0.0).then_inc(v_zero, 1)

            @block.tensor
            def _(pe):
                pe.wait_ge(loaded, 7 * 16)

                def scores(i, par, s):
                    hp, qt = s // 2, s % 2
                    if s == 0:
                        pe.wait_ge(qT_done, i + 1)
                        pe.wait_ge(kT_done, i * 2 + 2)
                        if not first(i):
                            pe.wait_ge(exp_done, i * 2 * NS)
                    if s >= 3:
                        pe.wait_ge(exp_done, i * 2 * NS + 2 * (s - 2))
                    u, r = hp // 4, 2 * hp % HPT
                    pe.matmul(SC[s % 3], qT[:, par, u, qt * P:(qt + 1) * P], kT[:, par, u, r:r + 2, :],
                              start=True, stop=True).then_inc(scores_done, 1)

                def turn_probs(i, s):
                    qt = s % 2
                    pe.wait_ge(probs_done, i * 2 * NS + 2 * (s + 1))
                    if s == 0 and not first(i):
                        pe.wait_ge(diag_done, i * NS)
                        pe.wait_ge(full_done, i * (NS // 2))
                    if s >= 2:
                        pe.wait_ge(diag_done, i * NS + s - 1)
                        if s >= 3:
                            pe.wait_ge(full_done, i * (NS // 2) + (s - 1) // 2)
                    for h in range(2):
                        for c in range(qt + 1):
                            last = pe.transpose(TR[s % 2][:, h, c, :], probs[:, s % 3, h, c * P:(c + 1) * P],
                                                ident[:, :])
                    last.then_inc(probsT_in_psum, 1)

                def weigh_values(i, par, hp):
                    u = hp // 4
                    pe.wait_ge(diag_done, i * NS + 2 * hp + 2)
                    pe.wait_ge(full_done, i * (NS // 2) + hp + 1)
                    for h in range(2):
                        r = (2 * hp + h) % HPT
                        for c in range(2):
                            last = pe.matmul(OT[u][:, c * P:T], v_pad[:, par, c, u, r * P:(r + 1) * P],
                                             probsT[:, hp % 2, h, c, c * P:T],
                                             start=(r == 0 and c == 0), stop=(r == HPT - 1 and c == 1),
                                             skip_group_check=True)
                    last.then_inc(av_done, 1)

                def turn_input(i):
                    pe.wait_ge(xn_done, i * 2 + 2)
                    if not first(i) and not first(i - 1):
                        pe.wait_ge(y_done, i - 1)
                    for n in range(2):
                        for c in range(KC):
                            last = pe.transpose(BANK[:, (c * 2 + n) * P:(c * 2 + n + 1) * P],
                                                xn[:, n, c * P:(c + 1) * P], ident[:, :])
                    last.then_inc(xT_in_psum, 1)

                def project_qk(i, n):
                    if n == 0:
                        pe.wait_ge(xT_done, i + 1)
                    else:
                        pe.wait_ge(qk_done, i * 6 + 1)
                    for c in range(KC):
                        last = pe.matmul(BANK, xT[:, c, n * P:(n + 1) * P], w_qkv[:, c, 0:2 * H],
                                         start=(c == 0), stop=(c == KC - 1))
                    last.then_inc(qkv_in_psum, 1)

                def project_v(i):
                    pe.wait_ge(qk_done, i * 6 + 2)
                    for n in range(2):
                        for c in range(KC):
                            last = pe.matmul(BANK[:, n * H:(n + 1) * H], xT[:, c, n * P:(n + 1) * P],
                                             w_qkv[:, c, 2 * H:3 * H], start=(c == 0), stop=(c == KC - 1))
                    last.then_inc(qkv_in_psum, 1)

                def turn_qk(i, part):
                    if part == 0:
                        pe.wait_ge(rope_done, i * 2 + 2)
                        pe.wait_ge(qk_done, i * 6 + 6)
                    else:
                        pe.wait_ge(qT_done, i + 1)
                    for n in range(2):
                        for u in range(2):
                            last = pe.transpose(QKT[:, u, n, :], qk[:, n, part * H + u * P:part * H + (u + 1) * P],
                                                ident[:, :])
                    last.then_inc(qkT_in_psum, 1)

                def project_out(i):
                    pe.wait_ge(oT_done, i * 2 + 2)
                    for n in range(2):
                        for c in range(KC):
                            last = pe.matmul(YB[:, n, :], oT[:, c, n * P:(n + 1) * P], w_o[:, c, :],
                                             start=(c == 0), stop=(c == KC - 1))
                    last.then_inc(y_in_psum, 1)

                def batch(i, par, ahead=True):
                    scores(i, par, 0)
                    for s in range(NS + 4):
                        if s + 1 < NS:
                            scores(i, par, s + 1)
                        if 2 <= s < NS + 2:
                            turn_probs(i, s - 2)
                        if s >= 4 and s % 2 == 0:
                            weigh_values(i, par, (s - 4) // 2)
                        if ahead:
                            if s == 3:
                                turn_input(i + 1)
                            if s == 5:
                                project_qk(i + 1, 0)
                            if s == 7:
                                project_qk(i + 1, 1)
                            if s == 9:
                                project_v(i + 1)
                            if s == 14:
                                turn_qk(i + 1, 0)
                            if s == 16:
                                turn_qk(i + 1, 1)
                        if s == 1 and not first(i):
                            project_out(i - 1)

                turn_input(0)
                project_qk(0, 0)
                project_qk(0, 1)
                project_v(0)
                turn_qk(0, 0)
                turn_qk(0, 1)
                batch(0, 0)
                with pe.Fori(0, B // 2 - 1) as i:
                    batch(2 * i + 1, 1)
                    batch(2 * i + 2, 0)
                batch(B - 1, 1, ahead=False)
                project_out(B - 1)

            @block.scalar
            def _(act):
                def exps(i, s):
                    act.wait_ge(max_done, i * NS + s + 1)
                    if s == 0 and not first(i):
                        act.wait_ge(probsT_in_psum, i * NS)
                    if s >= 3:
                        act.wait_ge(probsT_in_psum, i * NS + s - 2)
                    for h in range(2):
                        nc.scalar.activation(probs[:, s % 3, h, :], SC[s % 3][:, h, :], ACT.Exp,
                                             bias=neg_max[:, s % 4, h:h + 1],
                                             accum_out=row_sum[:, s % 4, h:h + 1]).then_inc(exp_done, 1)

                def full_block(i, hp):
                    act.wait_ge(diag_done, i * NS + 2 * hp + 2)
                    if hp >= 2 or not first(i):
                        act.wait_ge(av_done, i * (NS // 2) + hp - 1)
                    nc.scalar.copy(probsT[:, hp % 2, :, 0, P:T], TR[1][:, :, 0, :]).then_inc(full_done, 1)

                act.wait_ge(mv_done, NT)
                nc.scalar.activation(std[:, :], mv[:, :, 1], ACT.Sqrt, bias=k.eps[:, 0:1]).then_inc(std_done, 1)

                def copy_input(i):
                    act.wait_ge(xT_in_psum, i + 1)
                    nc.scalar.copy(xT[:, :, :], BANK.rearrange("p (c t) -> p c t", c=KC)).then_inc(xT_done, 1)

                def copy_q(i, par):
                    act.wait_ge(qkT_in_psum, i * 2 + 1)
                    nc.scalar.copy(qT[:, par], QKT.rearrange("p u n t -> p u (n t)")).then_inc(qT_done, 1)

                def batch(i, par, ahead=True):
                    for s in range(NS + 2):
                        if s < NS:
                            exps(i, s)
                        if s >= 3 and s % 2:
                            full_block(i, (s - 3) // 2)
                        if s == 11:
                            act.wait_ge(av_done, i * (NS // 2) + 4)
                            if not first(i):
                                act.wait_ge(y_in_psum, i)
                            nc.scalar.copy(oT[:, 0, :], OT[0]).then_inc(oT_done, 1)
                        if ahead and s == 4:
                            copy_input(i + 1)
                        if ahead and s == 15:
                            copy_q(i + 1, 1 - par)
                    act.wait_ge(av_done, i * (NS // 2) + 8)
                    nc.scalar.copy(oT[:, 1, :], OT[1]).then_inc(oT_done, 1)

                copy_input(0)
                copy_q(0, 0)
                batch(0, 0)
                with act.Fori(0, B // 2 - 1) as i:
                    batch(2 * i + 1, 1)
                    batch(2 * i + 2, 0)
                batch(B - 1, 1, ahead=False)

            @block.vector
            def _(dve):
                dve.wait_ge(loaded, 7 * 16)
                dve.wait_ge(v_zero, 1)

                def row_max(i, s):
                    dve.wait_ge(scores_done, i * NS + s + 1)
                    nc.vector.tensor_reduce(neg_max[:, s % 4, :], SC[s % 3], AX.X, ALU.max, negate=True)\
                        .then_inc(max_done, 1)

                def normalise(i, s):
                    dve.wait_ge(exp_done, i * 2 * NS + 2 * (s + 1))
                    nc.vector.reciprocal(row_inv[:, s % 4, :], row_sum[:, s % 4, :]).then_inc(inv_done, 1)
                    dve.wait_ge(inv_done, i * NS + s + 1)
                    for h in range(2):
                        p = probs[:, s % 3, h, :]
                        nc.vector.tensor_scalar(p, p, row_inv[:, s % 4, h:h + 1], None, ALU.mult)\
                            .then_inc(probs_done, 1)

                def diag_block(i, s):
                    hp, qt = s // 2, s % 2
                    dve.wait_ge(probsT_in_psum, i * NS + s + 1)
                    if qt == 0 and (hp >= 2 or not first(i)):
                        dve.wait_ge(av_done, i * (NS // 2) + hp - 1)
                    nc.vector.tensor_tensor(probsT[:, hp % 2, :, qt, qt * P:(qt + 1) * P],
                                            TR[s % 2][:, :, qt, :], bc(k.tri_incl[:, :], 1, 2), ALU.mult)\
                        .then_inc(diag_done, 1)

                for n in range(NT):
                    nc.vector.bn_stats(stats[:, n, :], X[:, n, :]).then_inc(stats_done, 1)
                dve.wait_ge(stats_done, NT)
                for n in range(NT):
                    nc.vector.bn_aggr(mv[:, n, :], stats[:, n, :]).then_inc(mv_done, 1)
                dve.wait_ge(std_done, 1)
                nc.vector.reciprocal(rstd[:, :], std[:, :]).then_inc(rstd_done, 1)
                dve.wait_ge(rstd_done, 1)

                def layer_norm(i):
                    if not first(i):
                        dve.wait_ge(xT_in_psum, i)
                    for n in range(2):
                        t = slice(n, n + 1) if first(i) else bass.ds(2 * i + n, 1)
                        nc.vector.tensor_scalar(xn[:, n, :], X[:, t, :], mv[:, t, 0], rstd[:, t],
                                                ALU.subtract, ALU.mult).then_inc(xn_done, 1)

                def add_qk_bias(i, n):
                    dve.wait_ge(qkv_in_psum, i * 3 + n + 1)
                    nc.vector.tensor_tensor(qk[:, n, :], BANK, b_qkv[:, 0:2 * H], ALU.add).then_inc(qk_done, 1)

                def place_v(i, par):
                    dve.wait_ge(qkv_in_psum, i * 3 + 3)
                    for n in range(2):
                        for u in range(2):
                            c0 = 2 * H + u * P
                            dst = v_pad[:, par, n, u, :].rearrange("p (r c) -> p r c", c=VPITCH)[:, :, 0:HSA]
                            nc.vector.tensor_tensor(
                                dst, BANK[:, n * H + u * P:n * H + (u + 1) * P].rearrange("p (r c) -> p r c", c=HSA),
                                b_qkv[:, c0:c0 + P].rearrange("p (r c) -> p r c", c=HSA), ALU.add).then_inc(qk_done, 1)

                def rotate(i, n):
                    dve.wait_ge(qk_done, i * 6 + 1 + n)
                    heads = qk[:, n, :].rearrange("p (a h c) -> p a h c", a=2, c=HSA)
                    for a in range(2):
                        nc.vector.tensor_tensor(
                            qk_cos[:, n, a * H:(a + 1) * H].rearrange("p (h c) -> p h c", c=HSA),
                            heads[:, a], bc(cos[:, n, a, :], 1, NHA), ALU.mult).then_inc(rope_parts, 1)
                        for e in range(2):
                            out = qk_sin[:, n, a * H:(a + 1) * H].rearrange("p (h e c) -> p h e c", e=2, c=8)
                            nc.vector.tensor_tensor(
                                out[:, :, e, :], heads[:, a, :, (1 - e) * 8:(2 - e) * 8],
                                bc(sin[:, n, a, e * 8:(e + 1) * 8], 1, NHA), ALU.mult).then_inc(rope_parts, 1)

                def rotated(i):
                    for n in range(2):
                        dve.wait_ge(rope_parts, i * 12 + 6 * (n + 1))
                        nc.vector.tensor_tensor(qk[:, n, :], qk_cos[:, n, :], qk_sin[:, n, :], ALU.add)\
                            .then_inc(rope_done, 1)

                def spread_k(i, par):
                    dve.wait_ge(qkT_in_psum, i * 2 + 2)
                    for u in range(2):
                        nc.vector.tensor_tensor(
                            kT[:, par, u, :, :], bc(QKT[:, u].rearrange("p n t -> p (n t)"), 1, HPT),
                            bc(head_rows[:, :], 2, T), ALU.mult).then_inc(kT_done, 1)

                def add_out(i):
                    dve.wait_ge(y_in_psum, i + 1)
                    nc.vector.tensor_tensor(y[:, :, :], YB, bc(b_o[:, :], 1, 2), ALU.add).then_inc(y_done, 1)
                    dve.wait_ge(y_done, i + 1)
                    xs = X[:, 0:2, :] if first(i) else X[:, bass.ds(2 * i, 2), :]
                    nc.vector.tensor_tensor(xs, xs, y[:, :, :], ALU.add).then_inc(x_done, 1)
                    dve.wait_ge(x_done, i + 1)

                def batch(i, par, ahead=True):
                    for s in range(NS + 2):
                        if s < NS:
                            row_max(i, s)
                        if 1 <= s < NS + 1:
                            normalise(i, s - 1)
                        if s >= 2:
                            diag_block(i, s - 2)
                        if ahead:
                            if s == 0:
                                layer_norm(i + 1)
                            if s in (6, 8):
                                add_qk_bias(i + 1, (s - 6) // 2)
                            if s in (9, 11):
                                rotate(i + 1, (s - 9) // 2)
                            if s == 10:
                                place_v(i + 1, 1 - par)
                            if s == 12:
                                rotated(i + 1)
                            if s == 17:
                                spread_k(i + 1, 1 - par)
                        if s == 2 and not first(i):
                            add_out(i - 1)

                layer_norm(0)
                add_qk_bias(0, 0)
                add_qk_bias(0, 1)
                place_v(0, 0)
                rotate(0, 0)
                rotate(0, 1)
                rotated(0)
                spread_k(0, 0)
                batch(0, 0)
                with dve.Fori(0, B // 2 - 1) as i:
                    batch(2 * i + 1, 1)
                    batch(2 * i + 2, 0)
                batch(B - 1, 1, ahead=False)
                add_out(B - 1)


def stage_moe(k, I_, run, bufs, outs):
    nc, X, ident, PS = k.nc, k.X, k.ident, k.PS
    EG = 4
    with semaphores(nc) as take, ExitStack() as ctx:
        def sb(name, shape, dt=F32):
            return ctx.enter_context(nc.sbuf_tensor(f"m{run}_{name}", shape, dt))

        def sem(name):
            return take(f"m{run}_{name}")

        xn = sb("xn", [P, NT, H])
        xT = sb("xT", [P, KC, B * T])
        w_router = sb("w_router", [P, KC, E])
        w_sg = sb("w_sg", [P, KC, IS])
        w_su = sb("w_su", [P, KC, IS])
        w_sd = sb("w_sd", [P, len(SHC), H])
        w_gu = sb("w_gu", [P, EG, KC * 2 * I])
        w_d = sb("w_d", [IH, EG, 2 * H])
        top_w = sb("top_w", [P, NT, 8])
        slot_in = sb("slot_in", [P, 2, NT], U32)
        slot_out = sb("slot_out", [P, 2, NT], U32)

        xT_done = sem("xT_done")
        shared_loaded = sem("shared_loaded")
        scattered = sem("scattered")
        gu_loaded = [sem(f"gu_loaded{j}") for j in range(EG)]
        d_loaded = [sem(f"d_loaded{j}") for j in range(EG)]

        def load_experts(sp, g, up_done, down_done):
            for j in range(EG):
                if up_done is not None:
                    sp.wait_ge(up_done, g * EG - EG + j + 1)
                sp.dma_start(w_gu[:, j:j + 1, :], I_["m_w_gu"].rearrange("e p n -> p e n")[:, bass.ds(g * EG + j, 1), :])\
                    .then_inc(gu_loaded[j], 16)
                if down_done is not None:
                    sp.wait_ge(down_done, g * EG - EG + j + 1)
                sp.dma_start(w_d[:, j:j + 1, :], I_["m_w_d"].rearrange("e p n -> p e n")[:, bass.ds(g * EG + j, 1), :])\
                    .then_inc(d_loaded[j], 16)

        TH = NT * P // 2
        NCH = len(SHC)
        UP = [(PS[:, 0, :], PS[:, 1, :]), (PS[:, 2, :], PS[:, 3, :])]
        s_gate = sb("s_gate", [P, 2, TH])
        s_h = sb("s_h", [P, NCH, TH])
        s_up_done = sem("s_up_done")
        s_silu_done = sem("s_silu_done")
        s_h_done = sem("s_h_done")
        s_y_done = sem("s_y_done")
        s_x_done = sem("s_x_done")

        def shared_products(pe, h):
            for q, (c0, m) in enumerate(SHC):
                if q >= 2:
                    pe.wait_ge(s_h_done, h * NCH + q - 1)
                for w, bank in zip((w_sg, w_su), UP[q % 2]):
                    for c in range(KC):
                        last = pe.matmul(bank[0:m, :], w[:, c, c0:c0 + m],
                                         xT[:, c, h * TH:(h + 1) * TH],
                                         start=(c == 0), stop=(c == KC - 1))
                last.then_inc(s_up_done, 1)
            pe.wait_ge(s_h_done, h * NCH + NCH)
            for n in range(4):
                for q, (c0, m) in enumerate(SHC):
                    last = pe.matmul(PS[:, 4 + n // 2, n % 2 * H:(n % 2 + 1) * H],
                                     s_h[0:m, q, n * P:(n + 1) * P], w_sd[0:m, q, :],
                                     start=(q == 0), stop=(q == NCH - 1))
                if n % 2:
                    last.then_inc(s_y_done, 1)

        def shared_silu(act, h):
            for q, (c0, m) in enumerate(SHC):
                act.wait_ge(s_up_done, h * NCH + q + 1)
                nc.scalar.activation(s_gate[0:m, q % 2, :], UP[q % 2][0][0:m, :], ACT.Silu)\
                    .then_inc(s_silu_done, 1)
                if q:
                    act.wait_ge(s_h_done, h * NCH + q)

        def shared_hidden(dve, h):
            for q, (c0, m) in enumerate(SHC):
                dve.wait_ge(s_silu_done, h * NCH + q + 1)
                nc.vector.tensor_tensor(s_h[0:m, q, :], s_gate[0:m, q % 2, :], UP[q % 2][1][0:m, :],
                                        ALU.mult).then_inc(s_h_done, 1)

        def shared_add(dve, h):
            for n in range(2):
                dve.wait_ge(s_y_done, h * 2 + n + 1)
                xs = X[:, h * 4 + 2 * n:h * 4 + 2 * n + 2, :]
                nc.vector.tensor_tensor(xs, xs, PS[:, 4 + n, :].rearrange("p (n d) -> p n d", n=2),
                                        ALU.add).then_inc(s_x_done, 1)

        with ExitStack() as c1:
            def sb1(name, shape, dt=F32):
                return c1.enter_context(nc.sbuf_tensor(f"m{run}_{name}", shape, dt))

            def sem1(name):
                return take(f"m{run}_{name}")

            stats = sb1("stats", [P, NT, 6])
            mv = sb1("mv", [P, NT, 2])
            std = sb1("std", [P, NT])
            rstd = sb1("rstd", [P, NT])
            expert_no = sb1("expert_no", [P, E])
            strict = sb1("strict", [P, P], BF16)
            ones = sb1("ones", [P, P], BF16)
            neg_max = sb1("neg_max", [P, NT])
            shifted = sb1("shifted", [P, NT, E])
            ex = sb1("ex", [P, NT, E])
            total = sb1("total", [P, NT])
            inv = sb1("inv", [P, NT])
            scores = sb1("scores", [P, NT, E])
            top_i = sb1("top_i", [P, NT, 8], U32)
            top_f = sb1("top_f", [P, 2, NT])
            chosen = sb1("chosen", [P, 2, NT, E])
            either = sb1("either", [P, NT, E], BF16)
            rank_of = sb1("rank_of", [P, 2, NT, E])
            rank = sb1("rank", [P, 2, NT])
            over = sb1("over", [P, 2, NT])
            far = sb1("far", [P, 2, NT])
            held = sb1("held", [P, 2, NT])

            router_loaded = sem1("router_loaded")
            const_ready = sem1("const_ready")
            stats_done = sem1("stats_done")
            mv_done = sem1("mv_done")
            std_done = sem1("std_done")
            rstd_done = sem1("rstd_done")
            xn_done = sem1("xn_done")
            xT_in_psum = sem1("xT_in_psum")
            logits_done = sem1("logits_done")
            exp_done = sem1("exp_done")
            step = sem1("route_step")
            either_done = sem1("either_done")
            rank_in_psum = sem1("rank_in_psum")
            slots_done = sem1("slots_done")

            LG = PS[:, 4, 0:NT * E].rearrange("p (n e) -> p n e", e=E)
            RK = PS[:, 5, 0:NT * E].rearrange("p (n e) -> p n e", e=E)

            with nc.Block() as block:

                @block.sync
                def _(sp):
                    sp.dma_start(w_router[:, :, :], I_["m_w_router"]).then_inc(router_loaded, 16)
                    sp.dma_start(expert_no[:, :], I_["m_expert_no"]).then_inc(router_loaded, 16)
                    for dst, name in ((w_sg, "m_w_sg"), (w_su, "m_w_su"), (w_sd, "m_w_sd")):
                        sp.dma_start(dst[:, :, :], I_[name]).then_inc(shared_loaded, 16)
                    load_experts(sp, 0, None, None)
                    sp.wait_ge(router_loaded, 32)

                @block.tensor
                def _(pe):
                    for n in range(NT):
                        pe.wait_ge(xn_done, n + 1)
                        if n % 2 == 0:
                            bank = PS[:, n // 2 % 4, :].rearrange("p (c t) -> p c t", c=KC)
                        for c in range(KC):
                            last = pe.transpose(bank[:, c, n % 2 * P:(n % 2 + 1) * P],
                                                xn[:, n, c * P:(c + 1) * P], ident[:, :])
                        last.then_inc(xT_in_psum, 1)
                    pe.wait_ge(router_loaded, 32)
                    for n in range(NT):
                        if n % 2 == 0:
                            pe.wait_ge(xT_done, n // 2 + 1)
                        for c in range(KC):
                            last = pe.matmul(LG[:, n, :], xT[:, c, n * P:(n + 1) * P], w_router[:, c, :],
                                             start=(c == 0), stop=(c == KC - 1))
                    last.then_inc(logits_done, 1)
                    pe.wait_ge(const_ready, 2)
                    pe.wait_ge(either_done, 1)
                    flat = either[:, :, :].rearrange("p n e -> p (n e)")
                    out = RK.rearrange("p n e -> p (n e)")
                    last = pe.matmul(out, strict[:, :], flat, start=True, stop=False, skip_group_check=True)
                    for m in range(1, NT):
                        last = pe.matmul(out[:, m * E:NT * E], ones[:, :], flat[:, 0:(NT - m) * E],
                                         start=False, stop=(m == NT - 1), skip_group_check=True)
                    last.then_inc(rank_in_psum, 1)

                @block.scalar
                def _(act):
                    act.wait_ge(mv_done, NT)
                    nc.scalar.activation(std[:, :], mv[:, :, 1], ACT.Sqrt, bias=k.eps[:, 0:1])\
                        .then_inc(std_done, 1)
                    for g in range(NT // 2):
                        act.wait_ge(xT_in_psum, 2 * g + 2)
                        nc.scalar.copy(xT[:, :, 2 * g * P:2 * (g + 1) * P],
                                       PS[:, g % 4, :].rearrange("p (c t) -> p c t", c=KC)).then_inc(xT_done, 1)
                    act.wait_ge(step, 2)
                    nc.scalar.activation(ex[:, :, :], shifted[:, :, :], ACT.Exp).then_inc(exp_done, 1)

                @block.vector
                def _(dve):
                    for n in range(NT):
                        nc.vector.bn_stats(stats[:, n, :], X[:, n, :]).then_inc(stats_done, 1)
                    dve.wait_ge(stats_done, NT)
                    for n in range(NT):
                        nc.vector.bn_aggr(mv[:, n, :], stats[:, n, :]).then_inc(mv_done, 1)
                    dve.wait_ge(std_done, 1)
                    nc.vector.reciprocal(rstd[:, :], std[:, :]).then_inc(rstd_done, 1)
                    dve.wait_ge(rstd_done, 1)
                    for n in range(NT):
                        nc.vector.tensor_scalar(xn[:, n, :], X[:, n, :], mv[:, n, 0:1], rstd[:, n:n + 1],
                                                ALU.subtract, ALU.mult).then_inc(xn_done, 1)
                    nc.vector.tensor_copy(strict[:, :], k.tri_strict[:, :]).then_inc(const_ready, 1)
                    dve.wait_ge(logits_done, 1)
                    nc.vector.tensor_reduce(neg_max[:, :], LG, AX.X, ALU.max, negate=True).then_inc(step, 1)
                    dve.wait_ge(step, 1)
                    nc.vector.tensor_tensor(shifted[:, :, :], LG, bc(neg_max[:, :], 2, E), ALU.add).then_inc(step, 1)
                    dve.wait_ge(exp_done, 1)
                    nc.vector.tensor_reduce(total[:, :], ex[:, :, :], AX.X, ALU.add).then_inc(step, 1)
                    dve.wait_ge(step, 3)
                    nc.vector.reciprocal(inv[:, :], total[:, :]).then_inc(step, 1)
                    dve.wait_ge(step, 4)
                    nc.vector.tensor_tensor(scores[:, :, :], ex[:, :, :], bc(inv[:, :], 2, E), ALU.mult).then_inc(step, 1)
                    dve.wait_ge(step, 5)
                    for n in range(NT):
                        nc.vector.max(top_w[:, n, :], scores[:, n, :]).then_inc(step, 1)
                    for n in range(NT):
                        dve.wait_ge(step, 6 + n)
                        nc.vector.max_index(top_i[:, n, :], top_w[:, n, :], scores[:, n, :]).then_inc(step, 1)
                    dve.wait_ge(step, 21)
                    nc.vector.tensor_copy(top_f[:, :, :], top_i[:, :, 0:2].rearrange("p n k -> p k n"))\
                        .then_inc(step, 1)
                    dve.wait_ge(step, 22)
                    dve.wait_ge(router_loaded, 32)
                    for q in range(2):
                        nc.vector.tensor_tensor(chosen[:, q], bc(expert_no[:, :], 1, NT), bc(top_f[:, q, :], 2, E),
                                                ALU.is_equal).then_inc(step, 1)
                    dve.wait_ge(step, 24)
                    nc.vector.tensor_tensor(either[:, :, :], chosen[:, 0], chosen[:, 1], ALU.add)\
                        .then_inc(either_done, 1)
                    dve.wait_ge(rank_in_psum, 1)
                    for q in range(2):
                        nc.vector.tensor_tensor(rank_of[:, q], RK, chosen[:, q], ALU.mult).then_inc(step, 1)
                    dve.wait_ge(step, 26)
                    nc.vector.tensor_reduce(rank[:, :, :], rank_of[:, :, :, :], AX.X, ALU.add).then_inc(step, 1)
                    dve.wait_ge(step, 27)
                    nc.vector.tensor_scalar(over[:, :, :], rank[:, :, :], float(CAP), float(2 * E * CAP),
                                            ALU.is_ge, ALU.mult).then_inc(step, 1)
                    nc.vector.tensor_scalar(held[:, :, :], rank[:, :, :], float(CAP - 1), None, ALU.min)\
                        .then_inc(step, 1)
                    dve.wait_ge(step, 28)
                    nc.vector.tensor_tensor(far[:, :, :], rank[:, :, :], over[:, :, :], ALU.add).then_inc(step, 1)
                    dve.wait_ge(step, 30)
                    for dst, r in ((slot_in, far), (slot_out, held)):
                        nc.vector.scalar_tensor_tensor(out=dst[:, :, :], in0=top_f[:, :, :], scalar=float(CAP),
                                                       in1=r[:, :, :], op0=ALU.mult, op1=ALU.add)\
                            .then_inc(slots_done, 1)

                @block.gpsimd
                def _(pool):
                    pool.memset(ones[:, :], 1.0).then_inc(const_ready, 1)

        with ExitStack() as c2:
            def sb2(name, shape, dt=F32):
                return c2.enter_context(nc.sbuf_tensor(f"m{run}_{name}", shape, dt))

            def sem2(name):
                return take(f"m{run}_{name}")

            rows = sb2("rows", [P, EG, H])
            rowsT = sb2("rowsT", [P, EG, KC, CAP])
            gate = sb2("gate", [P, EG, I])
            hid = sb2("hid", [P, EG, I])
            hidT = sb2("hidT", [IH, EG, 2, CAP])
            res = sb2("res", [P, EG, H])

            rows_loaded = [sem2(f"rows_loaded{j}") for j in range(EG)]
            rowsT_in_psum = sem2("rowsT_in_psum")
            rowsT_done = sem2("rowsT_done")
            up_done = sem2("up_done")
            silu_done = sem2("silu_done")
            hid_done = sem2("hid_done")
            hidT_in_psum = sem2("hidT_in_psum")
            hidT_done = sem2("hidT_done")
            down_done = sem2("down_done")
            res_done = sem2("res_done")
            stored = [sem2(f"stored{j}") for j in range(EG)]

            with nc.Block() as block:

                @block.gpsimd
                def _(pool):
                    for q in range(2):
                        for n in range(NT):
                            pool.indirect_dma_start(
                                out=bufs[:, :], out_offset=bass.IndirectOffsetOnAxis(ap=slot_in[:, q, n:n + 1], axis=0),
                                in_=xn[:, n, :], in_offset=None, bounds_check=E * CAP - 1,
                                oob_is_err=False).then_inc(scattered, 16)
                    pool.wait_ge(scattered, 16 * 2 * NT)

                @block.sync
                def _(sp):
                    def load_rows(g, j):
                        sp.dma_start(rows[:, j, :], bufs[bass.ds((g * EG + j) * CAP, CAP), :])\
                            .then_inc(rows_loaded[j], 16)

                    def store(g, j):
                        sp.wait_ge(res_done, EG + g * EG + j + 1)
                        sp.dma_start(outs[bass.ds((g * EG + j) * CAP, CAP), :], res[:, j, :])\
                            .then_inc(stored[j], 16)

                    sp.wait_ge(scattered, 16 * 2 * NT)
                    for j in range(EG):
                        load_rows(0, j)
                        sp.sem_inc(stored[j], 16)
                    with sp.Fori(1, E // EG) as step_no:
                        g = sp.snap(step_no)
                        for j in range(EG):
                            sp.wait_ge(rowsT_in_psum, g * EG - EG + j + 1)
                            load_rows(g, j)
                        load_experts(sp, g, up_done, down_done)
                        for j in range(EG):
                            store(g - 1, j)
                    for j in range(EG):
                        store(E // EG - 1, j)
                    for j in range(EG):
                        sp.wait_ge(stored[j], 16 + 16 * E // EG)

                @block.tensor
                def _(pe):
                    pe.wait_ge(shared_loaded, 48)
                    shared_products(pe, 0)
                    with pe.Fori(0, E // EG) as g:
                        for j in range(EG):
                            pe.wait_ge(rows_loaded[j], g * 16 + 16)
                            if j == 0:
                                pe.wait_ge(s_x_done, 2)
                            pe.wait_ge(res_done, g * EG + j + 1)
                            for c in range(KC):
                                last = pe.transpose(PS[:, 4 + j, c * P:(c + 1) * P],
                                                    rows[:, j, c * P:(c + 1) * P], ident[:, :])
                            last.then_inc(rowsT_in_psum, 1)
                        for j in range(EG):
                            pe.wait_ge(rowsT_done, g * EG + j + 1)
                            pe.wait_ge(gu_loaded[j], g * 16 + 16)
                            for c in range(KC):
                                last = pe.matmul(PS[:, j, 0:2 * I], rowsT[:, j, c, :], w_gu[:, j, c * 2 * I:(c + 1) * 2 * I],
                                                 start=(c == 0), stop=(c == KC - 1))
                            last.then_inc(up_done, 1)
                        for j in range(EG):
                            pe.wait_ge(hid_done, g * EG + j + 1)
                            for c in range(2):
                                last = pe.transpose(PS[0:IH, 4 + j, c * P:(c + 1) * P],
                                                    hid[:, j, c * IH:(c + 1) * IH], ident[:, :])
                            last.then_inc(hidT_in_psum, 1)
                        for j in range(EG):
                            pe.wait_ge(hidT_done, g * EG + j + 1)
                            pe.wait_ge(d_loaded[j], g * 16 + 16)
                            for c in range(2):
                                last = pe.matmul(PS[:, 4 + j, H:2 * H], hidT[:, j, c, :], w_d[:, j, c * H:(c + 1) * H],
                                                 start=(c == 0), stop=(c == 1))
                            last.then_inc(down_done, 1)

                @block.scalar
                def _(act):
                    shared_silu(act, 0)
                    with act.Fori(0, E // EG) as g:
                        for j in range(EG):
                            act.wait_ge(rowsT_in_psum, g * EG + j + 1)
                            nc.scalar.copy(rowsT[:, j, :, :],
                                           PS[:, 4 + j, 0:H].rearrange("p (c t) -> p c t", c=KC)).then_inc(rowsT_done, 1)
                        for j in range(EG):
                            act.wait_ge(up_done, g * EG + j + 1)
                            nc.scalar.activation(gate[:, j, :], PS[:, j, 0:I], ACT.Silu).then_inc(silu_done, 1)
                        for j in range(EG):
                            act.wait_ge(hidT_in_psum, g * EG + j + 1)
                            nc.scalar.copy(hidT[:, j, :, :],
                                           PS[0:IH, 4 + j, 0:2 * P].rearrange("p (c t) -> p c t", c=2))\
                                .then_inc(hidT_done, 1)

                @block.vector
                def _(dve):
                    shared_hidden(dve, 0)
                    shared_add(dve, 0)
                    dve.sem_inc(res_done, EG)
                    with dve.Fori(0, E // EG) as g:
                        for j in range(EG):
                            dve.wait_ge(silu_done, g * EG + j + 1)
                            nc.vector.tensor_tensor(hid[:, j, :], gate[:, j, :], PS[:, j, I:2 * I], ALU.mult)\
                                .then_inc(hid_done, 1)
                        for j in range(EG):
                            dve.wait_ge(down_done, g * EG + j + 1)
                            dve.wait_ge(stored[j], g * 16 + 16)
                            nc.vector.tensor_copy(res[:, j, :], PS[:, 4 + j, H:2 * H]).then_inc(res_done, 1)

        with ExitStack() as c3:
            got = c3.enter_context(nc.sbuf_tensor(f"m{run}_got", [P, NT, 2, H], F32))
            gathered = [take(f"m{run}_gathered{n}") for n in range(NT)]
            first_added = take(f"m{run}_first_added")
            second_added = take(f"m{run}_second_added")
            def second(dve, n):
                dve.wait_ge(first_added, n + 1)
                nc.vector.scalar_tensor_tensor(out=X[:, n, :], in0=got[:, n, 1, :], scalar=top_w[:, n, 1:2],
                                               in1=X[:, n, :], op0=ALU.mult, op1=ALU.add)\
                    .then_inc(second_added, 1)

            with nc.Block() as block:

                @block.gpsimd
                def _(pool):
                    for n in range(NT):
                        for q in range(2):
                            pool.indirect_dma_start(
                                out=got[:, n, q, :], out_offset=None, in_=outs[:, :],
                                in_offset=bass.IndirectOffsetOnAxis(ap=slot_out[:, q, n:n + 1], axis=0),
                                bounds_check=E * CAP - 1, oob_is_err=True).then_inc(gathered[n], 16)
                    for n in range(NT):
                        pool.wait_ge(gathered[n], 32)

                @block.tensor
                def _(pe):
                    shared_products(pe, 1)

                @block.scalar
                def _(act):
                    shared_silu(act, 1)

                @block.vector
                def _(dve):
                    shared_hidden(dve, 1)
                    for n in range(NT):
                        if n == NT // 2:
                            shared_add(dve, 1)
                            dve.wait_ge(s_x_done, 4)
                        dve.wait_ge(gathered[n], 32)
                        nc.vector.scalar_tensor_tensor(out=X[:, n, :], in0=got[:, n, 0, :], scalar=top_w[:, n, 0:1],
                                                       in1=X[:, n, :], op0=ALU.mult, op1=ALU.add)\
                            .then_inc(first_added, 1)
                        if n:
                            second(dve, n - 1)
                    second(dve, NT - 1)


LEVELS = [2, 4, 8, 16, 32]
NG = 4
WPAIR = KC * 4 * P + 3 * TAPS


def stage_delta(k, I_):
    nc, X, ident, PS = k.nc, k.X, k.ident, k.PS
    NL = len(LEVELS)
    with semaphores(nc) as take, ExitStack() as ctx:
        def sb(name, shape, dt=F32):
            return ctx.enter_context(nc.sbuf_tensor("d_" + name, shape, dt))

        def sem(name):
            return take("d_" + name)

        xT = sb("xT", [P, KC, B * T])
        w_pair = sb("w_pair", [P, 2, WPAIR])
        w_out = sb("w_out", [P, H])
        off_mask = sb("off_mask", [P, NL, P])
        pair_mask = sb("pair_mask", [P, P])
        after = sb("after", [P, P])
        neg_half = sb("neg_half", [P, 16])
        norm_eps = sb("norm_eps", [P, 16])
        o_eps = sb("o_eps", [P, 16])
        gate_w = sb("gate_w", [P, 1])
        beta = sb("beta", [P, NH, NT])
        g = sb("g", [P, NH, NT])
        grow = sb("grow", [P, NH, NT])
        rest = sb("rest", [P, NH, NT])

        setup_loaded = sem("setup_loaded")
        w_loaded = [sem(f"w_loaded{slot}") for slot in range(2)]
        wo_loaded = sem("wo_loaded")

        def w_src(p):
            return I_["d_w_pair"].rearrange("q p n -> p q n")[:, bass.ds(p, 1), :]

        def wo_src(p):
            return I_["d_w_out"].rearrange("q p n -> p q n")[:, bass.ds(p, 1), :]

        with ExitStack() as c1:
            def sb1(name, shape, dt=F32):
                return c1.enter_context(nc.sbuf_tensor("d_" + name, shape, dt))

            def sem1(name):
                return take("d_" + name)

            stats = sb1("stats", [P, NT, 6])
            mv = sb1("mv", [P, NT, 2])
            std = sb1("std", [P, NT])
            rstd = sb1("rstd", [P, NT])
            xn = sb1("xn", [P, NT, H])
            w_ba = sb1("w_ba", [P, KC, 2 * NH])
            a_log = sb1("a_log", [P, NH])
            dt_bias = sb1("dt_bias", [P, NH])
            norm_w = sb1("norm_w", [P, 1])
            exp_a = sb1("exp_a", [P, NH])
            s_in = sb1("s_in", [P, NT, NH])
            s_abs = sb1("s_abs", [P, NT, NH])
            s_exp = sb1("s_exp", [P, NT, NH])
            s_ln = sb1("s_ln", [P, NT, NH])
            soft = sb1("soft", [P, NT, NH])
            half_tanh = sb1("half_tanh", [P, NT, NH])

            stats_done = sem1("stats_done")
            mv_done = sem1("mv_done")
            std_done = sem1("std_done")
            rstd_done = sem1("rstd_done")
            xn_done = sem1("xn_done")
            xT_in_psum = sem1("xT_in_psum")
            xT_done = sem1("xT_done")
            ba_done = sem1("ba_done")
            gate_act = sem1("gate_act")
            gate_dve = sem1("gate_dve")
            sums_done = sem1("sums_done")
            BA = PS[:, 4, :].rearrange("p (n c) -> p n c", n=NT)

            with nc.Block() as block:

                @block.sync
                def _(sp):
                    sp.dma_start(w_ba[:, :, :], I_["d_w_ba"]).then_inc(setup_loaded, 16)
                    sp.dma_start(a_log[:, :], I_["d_a_log"].partition_broadcast(P)).then_inc(setup_loaded, 16)
                    sp.dma_start(dt_bias[:, :], I_["d_dt_bias"].partition_broadcast(P)).then_inc(setup_loaded, 16)
                    sp.dma_start(norm_w[:, :], I_["d_norm_w"]).then_inc(setup_loaded, 16)
                    sp.dma_start(after[:, :], I_["after"]).then_inc(setup_loaded, 16)
                    sp.dma_start(pair_mask[:, :], I_["pair_mask"]).then_inc(setup_loaded, 16)
                    sp.dma_start(off_mask[:, :, :], I_["off_mask"]).then_inc(setup_loaded, 16)
                    sp.wait_ge(setup_loaded, 7 * 16)

                @block.gpsimd
                def _(pool):
                    pool.memset(neg_half[:, :], -0.5)
                    pool.memset(norm_eps[:, 0:8], D * GEPS)
                    pool.memset(norm_eps[:, 8:16], GEPS)
                    pool.memset(o_eps[:, :], GEPS)

                @block.tensor
                def _(pe):
                    for n in range(NT):
                        pe.wait_ge(xn_done, n + 1)
                        bank = PS[:, n // 2, :].rearrange("p (c t) -> p c t", c=KC)
                        for c in range(KC):
                            last = pe.transpose(bank[:, c, n % 2 * P:(n % 2 + 1) * P],
                                                xn[:, n, c * P:(c + 1) * P], ident[:, :])
                        last.then_inc(xT_in_psum, 1)
                    pe.wait_ge(setup_loaded, 7 * 16)
                    for n in range(NT):
                        if n % 2 == 0:
                            pe.wait_ge(xT_done, n // 2 + 1)
                        for c in range(KC):
                            last = pe.matmul(BA[:, n, :], xT[:, c, n * P:(n + 1) * P], w_ba[:, c, :],
                                             start=(c == 0), stop=(c == KC - 1))
                    last.then_inc(ba_done, 1)
                    pe.wait_ge(gate_dve, 5)
                    flat = g[:, :, :].rearrange("p h n -> p (h n)")
                    pe.matmul(PS[:, 5, 0:NH * NT], k.tri_incl[:, :], flat, start=True, stop=True)
                    pe.matmul(PS[:, 5, NH * NT:2 * NH * NT], after[:, :], flat, start=True, stop=True)\
                        .then_inc(sums_done, 1)

                @block.scalar
                def _(act):
                    act.wait_ge(mv_done, NT)
                    nc.scalar.activation(std[:, :], mv[:, :, 1], ACT.Sqrt, bias=k.eps[:, 0:1])\
                        .then_inc(std_done, 1)
                    for q in range(NT // 2):
                        act.wait_ge(xT_in_psum, 2 * q + 2)
                        nc.scalar.copy(xT[:, :, 2 * q * P:2 * (q + 1) * P],
                                       PS[:, q, :].rearrange("p (c t) -> p c t", c=KC)).then_inc(xT_done, 1)
                    act.wait_ge(setup_loaded, 7 * 16)
                    nc.scalar.activation(exp_a[:, :], a_log[:, :], ACT.Exp).then_inc(gate_act, 1)
                    act.wait_ge(ba_done, 1)
                    nc.scalar.activation(half_tanh[:, :, :], BA[:, :, 0:NH], ACT.Tanh, scale=0.5)\
                        .then_inc(gate_act, 1)
                    act.wait_ge(gate_dve, 2)
                    nc.scalar.activation(s_abs[:, :, :], s_in[:, :, :], ACT.Abs).then_inc(gate_act, 1)
                    act.wait_ge(gate_act, 3)
                    nc.scalar.activation(s_exp[:, :, :], s_abs[:, :, :], ACT.Exp, scale=-1.0).then_inc(gate_act, 1)
                    act.wait_ge(gate_act, 4)
                    nc.scalar.activation(s_ln[:, :, :], s_exp[:, :, :], ACT.Ln, bias=1.0).then_inc(gate_act, 1)
                    act.wait_ge(sums_done, 1)
                    nc.scalar.activation(grow[:, :, :], PS[:, 5, 0:NH * NT].rearrange("p (h n) -> p h n", n=NT),
                                         ACT.Exp)
                    nc.scalar.activation(rest[:, :, :],
                                         PS[:, 5, NH * NT:2 * NH * NT].rearrange("p (h n) -> p h n", n=NT), ACT.Exp)

                @block.vector
                def _(dve):
                    for n in range(NT):
                        nc.vector.bn_stats(stats[:, n, :], X[:, n, :]).then_inc(stats_done, 1)
                    dve.wait_ge(stats_done, NT)
                    for n in range(NT):
                        nc.vector.bn_aggr(mv[:, n, :], stats[:, n, :]).then_inc(mv_done, 1)
                    dve.wait_ge(std_done, 1)
                    nc.vector.reciprocal(rstd[:, :], std[:, :]).then_inc(rstd_done, 1)
                    dve.wait_ge(rstd_done, 1)
                    for n in range(NT):
                        nc.vector.tensor_scalar(xn[:, n, :], X[:, n, :], mv[:, n, 0:1], rstd[:, n:n + 1],
                                                ALU.subtract, ALU.mult).then_inc(xn_done, 1)
                    dve.wait_ge(setup_loaded, 7 * 16)
                    nc.vector.tensor_scalar(gate_w[:, :], norm_w[:, :], 0.5, None, ALU.mult).then_inc(gate_dve, 1)
                    dve.wait_ge(gate_act, 2)
                    nc.vector.tensor_tensor(s_in[:, :, :], BA[:, :, NH:2 * NH], bc(dt_bias[:, :], 1, NT), ALU.add)\
                        .then_inc(gate_dve, 1)
                    nc.vector.tensor_scalar(beta[:, :, :].rearrange("p h n -> p n h"), half_tanh[:, :, :], 0.5, 0.5,
                                            ALU.mult, ALU.add).then_inc(gate_dve, 1)
                    dve.wait_ge(gate_act, 5)
                    dve.wait_ge(gate_dve, 3)
                    nc.vector.scalar_tensor_tensor(out=soft[:, :, :], in0=s_in[:, :, :], scalar=0.0,
                                                   in1=s_ln[:, :, :], op0=ALU.max, op1=ALU.add).then_inc(gate_dve, 1)
                    dve.wait_ge(gate_dve, 4)
                    nc.vector.scalar_tensor_tensor(out=g[:, :, :].rearrange("p h n -> p n h"), in0=soft[:, :, :],
                                                   scalar=-1.0, in1=bc(exp_a[:, :], 1, NT), op0=ALU.mult,
                                                   op1=ALU.mult).then_inc(gate_dve, 1)

        pad = sb("pad", [P, 3, B, PADT])
        conv = sb("conv", [P, 3, B, T])
        w_gated = sb("w_gated", [P, H])
        z_tanh = sb("z_tanh", [P, 2, NT, P])
        square = sb("square", [P, 2, 4, P])
        ssum = sb("ssum", [P, 4, 8])
        ssum_e = sb("ssum_e", [P, 4, 8])
        rnorm = sb("rnorm", [P, 4, 8])
        qk_tok = sb("qk_tok", [P, 2, NT, P])
        k_rest = sb("k_rest", [P, 2, B, P])
        v_tok = sb("v_tok", [P, 2, NT, P])
        qkT = sb("qkT", [P, 2, NT, 2, P])
        g_tri = sb("g_tri", [P, NG, B, P])
        decay = sb("decay", [P, NG, B, P])
        decay_incl = sb("decay_incl", [P, NG, B, P])
        LT = sb("LT", [P, NG, B, P])
        AT = sb("AT", [P, NG, B, P])
        TT = sb("TT", [P, NG, B, P])
        TN = sb("TN", [P, NG, B, P])
        joined = sb("joined", [P, NG, B, P])
        rows_of = sb("rows_of", [P, NG, B, D])
        u = sb("u", [P, NG, B, D])
        state = sb("state", [P, B, D])
        seen = sb("seen", [P, 2, B, 2, D])
        resid = sb("resid", [P, 2, B, D])
        o_tok = sb("o_tok", [P, NT, P])
        o_square = sb("o_square", [P, NT, P])
        o_sum = sb("o_sum", [P, 2 * NT])
        o_sum_e = sb("o_sum_e", [P, 2 * NT])
        o_rnorm = sb("o_rnorm", [P, 2 * NT])
        o_out = sb("o_out", [P, NT, P])
        oT = sb("oT", [P, B * T])

        pads_zero = sem("pads_zero")
        proj_done = sem("proj_done")
        pad_done = sem("pad_done")
        z_in_psum = sem("z_in_psum")
        z_tanh_done = sem("z_tanh_done")
        w_gated_done = sem("w_gated_done")
        conv_step = [sem(f"conv_step{j}") for j in range(3)]
        tok_in_psum = sem("tok_in_psum")
        square_done = sem("square_done")
        ssum_done = sem("ssum_done")
        ssum_e_done = sem("ssum_e_done")
        rnorm_done = sem("rnorm_done")
        qk_tok_done = sem("qk_tok_done")
        v_tok_done = sem("v_tok_done")
        k_rest_done = sem("k_rest_done")
        qkT_in_psum = sem("qkT_in_psum")
        qkT_done = sem("qkT_done")
        g_tri_done = sem("g_tri_done")
        decay_in_psum = sem("decay_in_psum")
        decay_done = sem("decay_done")
        masked_done = sem("masked_done")
        kk_in_psum = sem("kk_in_psum")
        LT_done = sem("LT_done")
        AT_done = sem("AT_done")
        picked_done = sem("picked_done")
        pairs_done = sem("pairs_done")
        TT_done = sem("TT_done")
        TN_in_psum = sem("TN_in_psum")
        TN_done = sem("TN_done")
        join_in_psum = sem("join_in_psum")
        joined_done = sem("joined_done")
        delta_in_psum = sem("delta_in_psum")
        first_in_psum = sem("first_in_psum")
        first_done = sem("first_done")
        carry_in_psum = sem("carry_in_psum")
        less_done = sem("less_done")
        u_in_psum = sem("u_in_psum")
        u_done = sem("u_done")
        state_in_psum = sem("state_in_psum")
        state_done = sem("state_done")
        seen_in_psum = sem("seen_in_psum")
        seen_done = sem("seen_done")
        resid_done = sem("resid_done")
        o_in_psum = sem("o_in_psum")
        o_tok_done = sem("o_tok_done")
        o_square_done = sem("o_square_done")
        o_sum_done = sem("o_sum_done")
        o_sum_e_done = sem("o_sum_e_done")
        o_rnorm_done = sem("o_rnorm_done")
        o_unit_done = sem("o_unit_done")
        o_out_done = sem("o_out_done")
        oT_in_psum = sem("oT_in_psum")
        oT_done = sem("oT_done")
        y_in_psum = sem("y_in_psum")
        x_done = sem("x_done")

        def four(bank):
            return PS[:, bank, :].rearrange("p (b t) -> p b t", b=4)

        G = [four(4 + q) for q in range(NG)]
        LOW, HIGH = slice(0, D), slice(D, P)

        with nc.Block() as block:

            @block.sync
            def _(sp):
                def load_pair(p, slot):
                    sp.dma_start(w_pair[:, slot, :].unsqueeze(1), w_src(p)).then_inc(w_loaded[slot], 16)

                load_pair(0, 0)
                load_pair(1, 1)
                sp.dma_start(w_out[:, :].unsqueeze(1), wo_src(0)).then_inc(wo_loaded, 16)
                with sp.Fori(1, NP // 2) as i:
                    for par in range(2):
                        p = sp.snap(2 * i + par)
                        z_count, before = sp.snap((p - 1) * 2), sp.snap(p - 1)
                        sp.wait_ge(z_in_psum, z_count)
                        load_pair(p, par)
                        sp.wait_ge(w_gated_done, before)
                        sp.dma_start(w_out[:, :].unsqueeze(1), wo_src(before)).then_inc(wo_loaded, 16)
                sp.wait_ge(w_gated_done, NP - 1)
                sp.dma_start(w_out[:, :].unsqueeze(1), wo_src(NP - 1)).then_inc(wo_loaded, 16)

            @block.tensor
            def _(pe):
                def pairs_to(n):
                    return min(n, NP) if isinstance(n, int) else n

                def project(p, par, m):
                    j, half = m // 2, m % 2
                    if m == 0:
                        pe.wait_ge(w_loaded[par], (p - par) * 8 + 16)
                    if m < 4:
                        after_qkT(p, m)
                    else:
                        pe.wait_ge(pad_done, p * 6 + m - 3)
                    for c in range(KC):
                        w0 = (c * 4 + j) * P
                        last = pe.matmul(PS[:, m % 4, :], w_pair[:, par, w0:w0 + P],
                                         xT[:, c, half * 512:(half + 1) * 512],
                                         start=(c == 0), stop=(c == KC - 1))
                    last.then_inc(proj_done, 1)

                def after_qkT(p, m):
                    if isinstance(p, int) and p == 1:
                        pe.wait_ge(AT_done, 2 * NG)
                    elif not (isinstance(p, int) and p == 0):
                        pe.wait_ge(qkT_done, (p - 1) * 4 + [3, 4, 1, 2][m])

                def project_z(p, par, m):
                    for n in range(4 * m, 4 * m + 4):
                        for c in range(KC):
                            w0 = (c * 4 + 3) * P
                            if n == 4 * m and c == 0:
                                pe.wait_ge(pad_done, pairs_to(p + 2) * 6)
                            last = pe.matmul(PS[:, 2 + m, n % 4 * P:(n % 4 + 1) * P],
                                             xT[:, c, n * P:(n + 1) * P], w_pair[:, par, w0:w0 + P],
                                             start=(c == 0), stop=(c == KC - 1))
                    last.then_inc(z_in_psum, 1)

                def to_tokens(p, m):
                    j, half = m // 2, m % 2
                    pe.wait_ge(conv_step[j], (p + 1) * TAPS)
                    if m < 4:
                        if isinstance(p, int) and p == 0:
                            pe.wait_ge(pad_done, 6)
                        elif isinstance(p, int) and p == 1:
                            pe.wait_ge(pad_done, 12)
                            pe.wait_ge(z_tanh_done, 2)
                        else:
                            pe.wait_ge(x_done, (p - 2) * 4 + m + 1)
                    else:
                        pe.wait_ge(qk_tok_done, p * 4 + m - 3)
                    flat = conv[:, j, :, :].rearrange("p b t -> p (b t)")
                    for n in range(4):
                        t0 = (4 * half + n) * P
                        last = pe.transpose(PS[:, m % 4, n * P:(n + 1) * P], flat[:, t0:t0 + P], ident[:, :])
                    last.then_inc(tok_in_psum, 1)

                def to_channels(p, m):
                    pe.wait_ge(qk_tok_done, p * 4 + [3, 4, 4, 4][m])
                    if m >= 2:
                        pe.wait_ge(v_tok_done, p * 2 + m - 1)
                    for n in range(4):
                        last = pe.transpose(PS[:, (m + 2) % 4, n * P:(n + 1) * P],
                                            qk_tok[:, m // 2, 4 * (m % 2) + n, :], ident[:, :])
                    last.then_inc(qkT_in_psum, 1)

                def decays(p, q):
                    pe.wait_ge(g_tri_done, p * NG + q + 1)
                    if isinstance(p, int) and p == 0:
                        pe.wait_ge(qkT_done, 4)
                    elif q == 0:
                        pe.wait_ge(pad_done, pairs_to(p + 2) * 6)
                        pe.wait_ge(z_tanh_done, p * 2 + 2)
                    pe.matmul(PS[:, q, :], after[:, :], g_tri[:, q, :, :].rearrange("p b t -> p (b t)"),
                              start=True, stop=True).then_inc(decay_in_psum, 1)

                def products_of(p, par, m):
                    q, pairb = m // 2, m % 2
                    hd, ch = q // 2, q % 2
                    if m < 4:
                        pe.wait_ge(decay_done, p * NG + m + 1)
                        if m == 0:
                            pe.wait_ge(qkT_done, p * 4 + 4)
                    else:
                        pe.wait_ge(AT_done, p * 2 * NG + m - 3)
                    for e in range(2):
                        n = 2 * (2 * pairb + e) + ch
                        rows = qkT[hd * D:(hd + 1) * D, par, n, :, :]
                        last = pe.matmul(PS[:, m % 4, e * 2 * P:(e + 1) * 2 * P], rows[:, 0, :],
                                         rows.rearrange("p a t -> p (a t)"), start=True, stop=True)
                    last.then_inc(kk_in_psum, 1)

                def turn(p, lv, q):
                    if lv == 0:
                        pe.wait_ge(pairs_done, p * NG + q + 1)
                    else:
                        pe.wait_ge(TT_done, (p * NL + lv - 1) * NG + q + 1)
                    for b in range(B):
                        last = pe.transpose(G[q][:, b, :], TT[:, q, b, :], ident[:, :])
                    last.then_inc(TN_in_psum, 1)

                def invert(p, par, ahead, behind):
                    if behind:
                        pe.wait_ge(o_tok_done, p * NG)
                    turn(p, 0, 0)
                    for lv in range(NL):
                        for q in range(NG):
                            if lv == 0 and q < NG - 1:
                                turn(p, 0, q + 1)
                            pe.wait_ge(TN_done, (p * NL + lv) * NG + q + 1)
                            for b in range(B):
                                last = pe.matmul(G[q][:, b, :], LT[:, q, b, :], TN[:, q, b, :],
                                                 start=True, stop=True)
                            last.then_inc(join_in_psum, 1)
                            if behind and lv == 1 and q in (1, 3):
                                turn_out(p - 1, q // 2)
                            if ahead and lv == 4:
                                if q < 2:
                                    to_tokens(p + 1, 4 + q)
                                else:
                                    to_channels(p + 1, q - 2)
                        for q in range(NG):
                            pe.wait_ge(joined_done, (p * NL + lv) * NG + q + 1)
                            for b in range(B):
                                last = pe.matmul(G[q][:, b, :], joined[:, q, b, :], TT[:, q, b, :],
                                                 start=True, stop=True)
                            last.then_inc(delta_in_psum, 1)
                            if behind and lv == 1:
                                project_out(p - 1, q)
                            if ahead and lv == 2:
                                to_tokens(p + 1, q)
                        if lv < NL - 1:
                            for q in range(NG):
                                turn(p, lv + 1, q)

                def solve_first(q, right):
                    for b in range(B):
                        to = slice(0, P) if b == 0 else LOW
                        last = pe.matmul(G[q][to, b, LOW], TT[LOW, q, b, to], right(b)[LOW], start=True, stop=True)
                    last.then_inc(first_in_psum, 1)

                def carry(p, q, nth):
                    pe.wait_ge(first_done, p * NG + nth + 1)
                    for b in range(B):
                        to = slice(0, P) if b == 0 else HIGH
                        last = pe.matmul(G[q][to, b, HIGH], LT[LOW, q, b, to], rows_of[LOW, q, b, :],
                                         start=True, stop=True)
                    last.then_inc(carry_in_psum, 1)

                def solve_last(p, q, nth):
                    pe.wait_ge(less_done, p * NG + nth + 1)
                    for b in range(B):
                        of = slice(0, P) if b == 0 else HIGH
                        last = pe.matmul(G[q][HIGH, b, LOW], TT[of, q, b, HIGH], rows_of[of, q, b, :],
                                         start=True, stop=True)
                    last.then_inc(u_in_psum, 1)

                def out_rows(q):
                    for b in range(B):
                        last = pe.matmul(G[q][:, b, 0:D], AT[:, q, b, :], u[:, q, b, :], start=True, stop=True)
                    last.then_inc(o_in_psum, 1)

                def recur(p, par, ahead2, ahead):
                    def run_ahead(m):
                        if ahead2:
                            project(p + 2, par, m)

                    for hd in range(2):
                        pe.wait_ge(TT_done, (p + 1) * NL * NG)
                        pe.wait_ge(v_tok_done, p * 2 + 2)
                        solve_first(2 * hd, lambda b: v_tok[:, par, 2 * b, hd * D:(hd + 1) * D])
                    if ahead:
                        to_channels(p + 1, 2)
                        to_channels(p + 1, 3)
                    run_ahead(0)
                    for hd in range(2):
                        carry(p, 2 * hd, hd)
                    run_ahead(1)
                    for hd in range(2):
                        solve_last(p, 2 * hd, hd)
                    run_ahead(2)
                    for hd in range(2):
                        q = 2 * hd
                        pe.wait_ge(u_done, p * NG + hd + 1)
                        pe.wait_ge(k_rest_done, p + 1)
                        for b in range(B):
                            last = pe.matmul(G[q + 1][hd * D:(hd + 1) * D, b, 0:D],
                                             k_rest[:, par, b, hd * D:(hd + 1) * D], u[:, q, b, :],
                                             start=True, stop=True)
                        last.then_inc(state_in_psum, 1)
                    for hd in range(2):
                        out_rows(2 * hd)
                    for hd in range(2):
                        q = 2 * hd + 1
                        pe.wait_ge(state_done, p * 2 + hd + 1)
                        for b in range(B):
                            for a in range(2):
                                rows = slice(hd * D, (hd + 1) * D)
                                last = pe.matmul(G[q][:, b, a * D:(a + 1) * D], qkT[rows, par, 2 * b + 1, a, :],
                                                 state[rows, b, :], start=True, stop=True)
                        last.then_inc(seen_in_psum, 1)
                    run_ahead(3)
                    for hd in range(2):
                        pe.wait_ge(resid_done, p * 2 + hd + 1)
                        solve_first(2 * hd + 1, lambda b: resid[:, hd, b, :])
                    run_ahead(4)
                    for hd in range(2):
                        carry(p, 2 * hd + 1, 2 + hd)
                    run_ahead(5)
                    for hd in range(2):
                        solve_last(p, 2 * hd + 1, 2 + hd)
                    if ahead:
                        for m in range(2):
                            project_z(p + 1, 1 - par, m)
                        for q in range(NG):
                            decays(p + 1, q)
                    for hd in range(2):
                        pe.wait_ge(u_done, p * NG + 2 + hd + 1)
                        out_rows(2 * hd + 1)

                def turn_out(p, m):
                    if m == 0:
                        pe.wait_ge(AT_done, pairs_to(p + 2) * 2 * NG)
                    pe.wait_ge(o_out_done, p * 2 + m + 1)
                    for n in range(4 * m, 4 * m + 4):
                        last = pe.transpose(PS[:, m, n % 4 * P:(n % 4 + 1) * P], o_out[:, n, :], ident[:, :])
                    last.then_inc(oT_in_psum, 1)

                def project_out(p, m):
                    if m == 0:
                        pe.wait_ge(w_gated_done, p + 1)
                        pe.wait_ge(oT_done, p * 2 + 2)
                    for n in (2 * m, 2 * m + 1):
                        last = pe.matmul(PS[:, m, n % 2 * H:(n % 2 + 1) * H], oT[:, n * P:(n + 1) * P],
                                         w_gated[:, :], start=True, stop=True)
                    last.then_inc(y_in_psum, 1)

                def products(p, par):
                    for m in range(2 * NG):
                        products_of(p, par, m)

                def pair(p, par, ahead2=True, ahead=True, behind=True):
                    invert(p, par, ahead, behind)
                    recur(p, par, ahead2, ahead)
                    if ahead:
                        products(p + 1, 1 - par)

                for m in range(6):
                    project(0, 0, m)
                for m in range(6):
                    to_tokens(0, m)
                for m in range(4):
                    to_channels(0, m)
                for q in range(NG):
                    decays(0, q)
                products(0, 0)
                for m in range(6):
                    project(1, 1, m)
                for m in range(2):
                    project_z(0, 0, m)
                pair(0, 0, behind=False)
                with pe.Fori(0, NP // 2 - 2) as i:
                    pair(2 * i + 1, 1)
                    pair(2 * i + 2, 0)
                pair(NP - 3, 1)
                pair(NP - 2, 0, ahead2=False)
                pair(NP - 1, 1, ahead2=False, ahead=False)
                for m in range(2):
                    turn_out(NP - 1, m)
                for m in range(4):
                    project_out(NP - 1, m)

            @block.scalar
            def _(act):
                def copy_projected(p, m):
                    j, half = m // 2, m % 2
                    if m % 2 == 0 and not (isinstance(p, int) and p == 0):
                        act.wait_ge(conv_step[j], p * TAPS)
                    act.wait_ge(proj_done, p * 6 + m + 1)
                    nc.scalar.copy(pad[:, j, 2 * half:2 * half + 2, TAPS - 1:PADT],
                                   PS[:, m % 4, :].rearrange("p (b t) -> p b t", b=2)).then_inc(pad_done, 1)

                def tanh_z(p, par, m):
                    act.wait_ge(z_in_psum, p * 2 + m + 1)
                    nc.scalar.activation(z_tanh[:, par, 4 * m:4 * m + 4, :], four(2 + m), ACT.Tanh, scale=0.5)\
                        .then_inc(z_tanh_done, 1)

                def square_of(p, m):
                    act.wait_ge(tok_in_psum, p * 6 + m + 1)
                    if not (isinstance(p, int) and p == 0 and m < 2):
                        act.wait_ge(ssum_done, p * 4 + m - 1)
                    nc.scalar.activation(square[:, m % 2], four(m), ACT.Square,
                                         scale=float(D) ** 0.5 if m < 2 else 1.0).then_inc(square_done, 1)

                def copy_v(p, par, m):
                    act.wait_ge(tok_in_psum, p * 6 + 5 + m)
                    nc.scalar.copy(v_tok[:, par, 4 * m:4 * m + 4, :], four(m)).then_inc(v_tok_done, 1)

                def copy_qkT(p, par, m):
                    act.wait_ge(qkT_in_psum, p * 4 + m + 1)
                    nc.scalar.copy(qkT[:, par, 4 * (m % 2):4 * (m % 2) + 4, 1 - m // 2, :], four((m + 2) % 4))\
                        .then_inc(qkT_done, 1)

                def first_tap(p, par, j):
                    w0 = KC * 4 * P + j * TAPS + TAPS - 1
                    if not (isinstance(p, int) and p == 0):
                        act.wait_ge(tok_in_psum, (p - 1) * 6 + 2 * j + 2)
                    act.wait_ge(pad_done, p * 6 + 2 * j + 2)
                    nc.scalar.activation(conv[:, j], pad[:, j, :, TAPS - 1:TAPS - 1 + T], ACT.Copy,
                                         scale=w_pair[:, par, w0:w0 + 1]).then_inc(conv_step[j], 1)

                def exp_decay(p, q):
                    act.wait_ge(decay_in_psum, p * NG + q + 1)
                    nc.scalar.activation(decay[:, q], four(q), ACT.Exp).then_inc(decay_done, 1)

                def invert(p, par, ahead, behind):
                    for lv in range(NL):
                        for q in range(NG):
                            act.wait_ge(TN_in_psum, (p * NL + lv) * NG + q + 1)
                            nc.scalar.copy(TN[:, q], G[q]).then_inc(TN_done, 1)
                            if ahead and lv in (0, 1, 2) and q == 1:
                                first_tap(p + 1, 1 - par, lv)
                        if behind and lv == 1:
                            copy_oT(p - 1)
                        if ahead and lv in (2, 3):
                            for m in range(2):
                                square_of(p + 1, 2 * (lv - 2) + m)
                        if ahead and lv == 4:
                            for m in range(2):
                                copy_v(p + 1, 1 - par, m)
                            for m in range(2):
                                copy_qkT(p + 1, 1 - par, m)

                def copy_first(p, q, nth):
                    act.wait_ge(first_in_psum, p * NG + nth + 1)
                    nc.scalar.copy(rows_of[LOW, q], G[q][LOW, :, LOW]).then_inc(first_done, 1)

                def recur(p, par, ahead2, ahead):
                    def run_ahead(m):
                        if ahead2:
                            copy_projected(p + 2, m)

                    for hd in range(2):
                        copy_first(p, 2 * hd, hd)
                    if ahead:
                        for m in range(2, 4):
                            copy_qkT(p + 1, 1 - par, m)
                    run_ahead(0)
                    run_ahead(1)
                    for hd in range(2):
                        rows = slice(hd * D, (hd + 1) * D)
                        act.wait_ge(state_in_psum, p * 2 + hd + 1)
                        nc.scalar.copy(state[rows, :, :], G[2 * hd + 1][rows, :, 0:D]).then_inc(state_done, 1)
                    run_ahead(2)
                    for hd in range(2):
                        copy_first(p, 2 * hd + 1, 2 + hd)
                    for m in range(3, 6):
                        run_ahead(m)
                    act.wait_ge(wo_loaded, p * 16 + 16)
                    nc.scalar.activation(w_gated[:, :], w_out[:, :], ACT.Copy, scale=gate_w[:, 0:1])\
                        .then_inc(w_gated_done, 1)
                    if ahead:
                        for m in range(2):
                            tanh_z(p + 1, 1 - par, m)
                        for q in range(NG):
                            exp_decay(p + 1, q)
                    act.wait_ge(o_tok_done, p * NG + NG)
                    nc.scalar.activation(o_square[:, :, :], o_tok[:, :, :], ACT.Square,
                                         scale=float(D) ** -0.5).then_inc(o_square_done, 1)

                def copy_oT(p):
                    for m in range(2):
                        act.wait_ge(oT_in_psum, p * 2 + m + 1)
                        nc.scalar.copy(oT[:, 512 * m:512 * (m + 1)], PS[:, m, :]).then_inc(oT_done, 1)

                def pair(p, par, ahead2=True, ahead=True, behind=True):
                    invert(p, par, ahead, behind)
                    recur(p, par, ahead2, ahead)

                act.wait_ge(pads_zero, 1)
                for j in range(3):
                    copy_projected(0, 2 * j)
                    copy_projected(0, 2 * j + 1)
                    first_tap(0, 0, j)
                for m in range(4):
                    square_of(0, m)
                for m in range(2):
                    copy_v(0, 0, m)
                for m in range(4):
                    copy_qkT(0, 0, m)
                for q in range(NG):
                    exp_decay(0, q)
                for m in range(6):
                    copy_projected(1, m)
                for m in range(2):
                    tanh_z(0, 0, m)
                pair(0, 0, behind=False)
                with act.Fori(0, NP // 2 - 2) as i:
                    pair(2 * i + 1, 1)
                    pair(2 * i + 2, 0)
                pair(NP - 3, 1)
                pair(NP - 2, 0, ahead2=False)
                pair(NP - 1, 1, ahead2=False, ahead=False)
                copy_oT(NP - 1)

            @block.vector
            def _(dve):
                def conv_tap(p, par, j, step):
                    tap = TAPS - 1 - step
                    w0 = KC * 4 * P + j * TAPS + tap
                    dve.wait_ge(conv_step[j], p * TAPS + step)
                    nc.vector.scalar_tensor_tensor(
                        out=conv[:, j], in0=pad[:, j, :, tap:tap + T], scalar=w_pair[:, par, w0:w0 + 1],
                        in1=conv[:, j], op0=ALU.mult, op1=ALU.add).then_inc(conv_step[j], 1)

                def lengths(p, m):
                    dve.wait_ge(square_done, p * 4 + m + 1)
                    nc.vector.tensor_reduce(ssum[:, m, :], square[:, m % 2].rearrange("p n (h d) -> p (n h) d", h=2),
                                            AX.X, ALU.add).then_inc(ssum_done, 1)

                def unit(p, m):
                    dve.wait_ge(rnorm_done, p * 4 + m + 1)
                    nc.vector.tensor_tensor(
                        qk_tok[:, m // 2, 4 * (m % 2):4 * (m % 2) + 4, :].rearrange("p n (h d) -> p (n h) d", h=2),
                        PS[:, m, :].rearrange("p (a d) -> p a d", d=D), bc(rnorm[:, m, :], 2, D),
                        ALU.mult).then_inc(qk_tok_done, 1)

                def weigh_kk(p, m):
                    q, pairb = m // 2, m % 2
                    hd, ch = q // 2, q % 2
                    dve.wait_ge(kk_in_psum, p * 2 * NG + m + 1)
                    dve.wait_ge(decay_done, p * NG + q + 1)
                    prod = PS[:, m % 4, :].rearrange("p (e a t) -> p e a t", e=2, a=2)
                    for e in range(2):
                        b = 2 * pairb + e
                        bt = beta[:, bass.ds(2 * p + hd, 1), 2 * b + ch]
                        nc.vector.scalar_tensor_tensor(out=LT[:, q, b, :], in0=prod[:, e, 0, :], scalar=bt,
                                                       in1=decay[:, q, b, :], op0=ALU.mult,
                                                       op1=ALU.mult).then_inc(LT_done, 1)

                def weigh_qk(p, m):
                    q, pairb = m // 2, m % 2
                    dve.wait_ge(masked_done, p * NG + q + 1)
                    prod = PS[:, m % 4, :].rearrange("p (e a t) -> p e a t", e=2, a=2)
                    nc.vector.tensor_tensor(AT[:, q, 2 * pairb:2 * pairb + 2, :], prod[:, :, 1, :],
                                            decay_incl[:, q, 2 * pairb:2 * pairb + 2, :], ALU.mult)\
                        .then_inc(AT_done, 1)

                def pick_pairs(p, q):
                    dve.wait_ge(LT_done, (p * NG + q) * B + B)
                    nc.vector.tensor_tensor(TT[:, q], LT[:, q], bc(pair_mask[:, :], 1, B), ALU.mult)\
                        .then_inc(picked_done, 1)

                def sum_out(p):
                    dve.wait_ge(o_square_done, p + 1)
                    nc.vector.tensor_reduce(o_sum[:, :], o_square[:, :, :].rearrange("p n (h d) -> p (n h) d", h=2),
                                            AX.X, ALU.add).then_inc(o_sum_done, 1)

                def products(p):
                    for q in range(NG):
                        weigh_kk(p, 2 * q)
                        weigh_kk(p, 2 * q + 1)
                        pick_pairs(p, q)
                        weigh_qk(p, 2 * q)
                        weigh_qk(p, 2 * q + 1)
                        if q == 1 and not (isinstance(p, int) and p == 0):
                            sum_out(p - 1)

                def invert(p, par, ahead, behind):
                    for lv in range(NL):
                        for q in range(NG):
                            dve.wait_ge(join_in_psum, (p * NL + lv) * NG + q + 1)
                            nc.vector.tensor_tensor(joined[:, q], G[q], bc(off_mask[:, lv, :], 1, B), ALU.mult)\
                                .then_inc(joined_done, 1)
                            if ahead and lv in (0, 1, 3) and q > 0:
                                conv_tap(p + 1, 1 - par, min(lv, 2), q)
                            if behind and lv == 2:
                                add_out(p - 1, q)
                            if ahead and lv == 3 and q in (0, 2):
                                unit(p + 1, q // 2)
                            if ahead and lv == 4 and q < 2:
                                unit(p + 1, 2 + q)
                        for q in range(NG):
                            dve.wait_ge(delta_in_psum, (p * NL + lv) * NG + q + 1)
                            nc.vector.tensor_tensor(TT[:, q], TT[:, q], G[q], ALU.subtract).then_inc(TT_done, 1)
                        if behind and lv == 0:
                            gate_out(p - 1, 1 - par)
                        if ahead and lv in (2, 3):
                            for m in range(2):
                                lengths(p + 1, 2 * (lv - 2) + m)

                def by_head(t, p, hd, ch):
                    return bc(t[:, bass.ds(2 * p + hd, 1), ch:NT:2].rearrange("p o n -> p (o n)"), 2, D)

                def less_carry(p, q, nth, right):
                    dve.wait_ge(carry_in_psum, p * NG + nth + 1)
                    nc.vector.tensor_tensor(rows_of[HIGH, q], right, G[q][HIGH, :, HIGH], ALU.subtract)\
                        .then_inc(less_done, 1)

                def scale_u(p, hd, ch):
                    dve.wait_ge(u_in_psum, p * NG + 2 * ch + hd + 1)
                    nc.vector.tensor_tensor(u[:, 2 * hd + ch], G[2 * hd + ch][:, :, 0:D], by_head(beta, p, hd, ch),
                                            ALU.mult).then_inc(u_done, 1)

                def recur(p, par):
                    heads = [slice(hd * D, (hd + 1) * D) for hd in range(2)]
                    for hd in range(2):
                        less_carry(p, 2 * hd, hd, v_tok[HIGH, par, 0:NT:2, heads[hd]])
                    for hd in range(2):
                        scale_u(p, hd, 0)
                    for hd in range(2):
                        dve.wait_ge(o_in_psum, p * NG + hd + 1)
                        nc.vector.tensor_copy(o_tok[:, 0:NT:2, heads[hd]], G[2 * hd][:, :, 0:D])\
                            .then_inc(o_tok_done, 1)
                    for hd in range(2):
                        dve.wait_ge(seen_in_psum, p * 2 + hd + 1)
                        dec = bc(grow[:, bass.ds(2 * p + hd, 1), 1:NT:2].rearrange("p o n -> p (o n)"), 2, 2 * D)
                        nc.vector.tensor_tensor(seen[:, hd].rearrange("p b a d -> p b (a d)"), G[2 * hd + 1],
                                                dec, ALU.mult).then_inc(seen_done, 1)
                        dve.wait_ge(seen_done, p * 2 + hd + 1)
                        nc.vector.tensor_tensor(resid[:, hd], v_tok[:, par, 1:NT:2, heads[hd]],
                                                seen[:, hd, :, 0, :], ALU.subtract).then_inc(resid_done, 1)
                    for hd in range(2):
                        less_carry(p, 2 * hd + 1, 2 + hd, resid[HIGH, hd])
                    for hd in range(2):
                        scale_u(p, hd, 1)
                    for hd in range(2):
                        dve.wait_ge(o_in_psum, p * NG + 2 + hd + 1)
                        nc.vector.tensor_tensor(o_tok[:, 1:NT:2, heads[hd]], G[2 * hd + 1][:, :, 0:D],
                                                seen[:, hd, :, 1, :], ALU.add).then_inc(o_tok_done, 1)

                def gate_out(p, par):
                    dve.wait_ge(o_unit_done, p + 1)
                    for m in range(2):
                        nc.vector.scalar_tensor_tensor(out=o_out[:, 4 * m:4 * m + 4, :],
                                                       in0=z_tanh[:, par, 4 * m:4 * m + 4, :], scalar=1.0,
                                                       in1=o_out[:, 4 * m:4 * m + 4, :], op0=ALU.add,
                                                       op1=ALU.mult).then_inc(o_out_done, 1)

                def add_out(p, m):
                    dve.wait_ge(y_in_psum, p * 4 + m + 1)
                    xs = X[:, 2 * m:2 * m + 2, :]
                    nc.vector.tensor_tensor(xs, xs, PS[:, m, :].rearrange("p (n d) -> p n d", n=2), ALU.add)\
                        .then_inc(x_done, 1)

                def pair(p, par, ahead=True, behind=True):
                    invert(p, par, ahead, behind)
                    recur(p, par)
                    if ahead:
                        products(p + 1)
                    else:
                        sum_out(p)

                for j in range(3):
                    for step in range(1, TAPS):
                        conv_tap(0, 0, j, step)
                for m in range(5):
                    if m < 4:
                        lengths(0, m)
                    if m:
                        unit(0, m - 1)
                products(0)
                pair(0, 0, behind=False)
                with dve.Fori(0, NP // 2 - 2) as i:
                    pair(2 * i + 1, 1)
                    pair(2 * i + 2, 0)
                pair(NP - 3, 1)
                pair(NP - 2, 0)
                pair(NP - 1, 1, ahead=False)
                gate_out(NP - 1, 1)
                for m in range(4):
                    add_out(NP - 1, m)

            @block.gpsimd
            def _(pool):
                def make_g_tri(p, q):
                    hd, ch = q // 2, q % 2
                    if not (isinstance(p, int) and p == 0):
                        pool.wait_ge(decay_in_psum, (p - 1) * NG + q + 1)
                    col = g[:, bass.ds(2 * p + hd, 1), ch:NT:2].rearrange("p o n -> p (o n)")
                    pool.tensor_tensor(g_tri[:, q], bc(k.tri_incl[:, :], 1, B), bc(col, 2, P), ALU.mult)\
                        .then_inc(g_tri_done, 1)

                def inverse_lengths(p, m):
                    pool.wait_ge(ssum_done, p * 4 + m + 1)
                    pool.tensor_tensor(ssum_e[:, m, :], ssum[:, m, :], norm_eps[:, 8 * (m // 2):8 * (m // 2) + 8],
                                       ALU.add).then_inc(ssum_e_done, 1)
                    pool.wait_ge(ssum_e_done, p * 4 + m + 1)
                    pool.tensor_tensor(rnorm[:, m, :], ssum_e[:, m, :], neg_half[:, 0:8], ALU.pow)\
                        .then_inc(rnorm_done, 1)

                def decay_k(p, par):
                    pool.wait_ge(qk_tok_done, p * 4 + 4)
                    for hd in range(2):
                        col = rest[:, bass.ds(2 * p + hd, 1), 0:NT:2].rearrange("p o n -> p (o n)")
                        last = pool.tensor_tensor(k_rest[:, par, :, hd * D:(hd + 1) * D],
                                                  qk_tok[:, 1, 0:NT:2, hd * D:(hd + 1) * D], bc(col, 2, D), ALU.mult)
                    last.then_inc(k_rest_done, 1)

                def mask_decay(p, q):
                    pool.wait_ge(decay_done, p * NG + q + 1)
                    pool.tensor_tensor(decay_incl[:, q], decay[:, q], bc(k.tri_incl[:, :], 1, B), ALU.mult)\
                        .then_inc(masked_done, 1)

                def invert_pairs(p, q):
                    pool.wait_ge(picked_done, p * NG + q + 1)
                    pool.tensor_tensor(TT[:, q], bc(ident[:, :], 1, B), TT[:, q], ALU.subtract)\
                        .then_inc(pairs_done, 1)

                def ready_decays(p):
                    for q in range(NG):
                        mask_decay(p, q)

                def norm_out(p):
                    pool.wait_ge(o_sum_done, p + 1)
                    pool.tensor_tensor(o_sum_e[:, :], o_sum[:, :], o_eps[:, :], ALU.add)\
                        .then_inc(o_sum_e_done, 1)
                    pool.wait_ge(o_sum_e_done, p + 1)
                    pool.tensor_tensor(o_rnorm[:, :], o_sum_e[:, :], neg_half[:, :], ALU.pow)\
                        .then_inc(o_rnorm_done, 1)
                    pool.wait_ge(o_rnorm_done, p + 1)
                    pool.tensor_tensor(o_out[:, :, :].rearrange("p n (h d) -> p (n h) d", h=2),
                                       o_tok[:, :, :].rearrange("p n (h d) -> p (n h) d", h=2),
                                       bc(o_rnorm[:, :], 2, D), ALU.mult).then_inc(o_unit_done, 1)

                def pair(p, par, ahead=True):
                    if ahead:
                        for m in range(4):
                            inverse_lengths(p + 1, m)
                        decay_k(p + 1, 1 - par)
                        for q in range(NG):
                            make_g_tri(p + 1, q)
                        ready_decays(p + 1)
                        for q in range(NG):
                            invert_pairs(p + 1, q)
                    norm_out(p)

                pool.memset(pad[:, :, :, :], 0.0).then_inc(pads_zero, 1)
                for q in range(NG):
                    make_g_tri(0, q)
                for m in range(4):
                    inverse_lengths(0, m)
                decay_k(0, 0)
                ready_decays(0)
                for q in range(NG):
                    invert_pairs(0, q)
                pair(0, 0)
                with pool.Fori(0, NP // 2 - 2) as i:
                    pair(2 * i + 1, 1)
                    pair(2 * i + 2, 0)
                pair(NP - 3, 1)
                pair(NP - 2, 0)
                pair(NP - 1, 1, ahead=False)


def build(nc, I_, out):
    k = Core()
    k.nc = nc
    k.bufs = [nc.dram_tensor(f"slot_rows{run}", [E * CAP, H], F32).ap() for run in range(2)]
    results = [nc.dram_tensor(f"slot_results{run}", [E * CAP, H], F32).ap() for run in range(2)]
    with ExitStack() as ctx:
        def sb(name, shape):
            return ctx.enter_context(nc.sbuf_tensor(name, shape, F32))

        k.X = sb("residual", [P, NT, H])
        k.ident = sb("ident", [P, P])
        k.tri_incl = sb("tri_incl", [P, P])
        k.tri_strict = sb("tri_strict", [P, P])
        k.eps = sb("ln_eps", [P, 1])
        k.PS = ctx.enter_context(nc.psum_tensor("psum", [P, 8, 512], F32))
        stage_load(k, I_)
        stage_attention_a(k, I_)
        stage_moe(k, I_, 0, k.bufs[0], results[0])
        stage_delta(k, I_)
        stage_moe(k, I_, 1, k.bufs[1], results[1])
        with semaphores(nc) as take, nc.Block() as block:
            stored = take("stored_out")

            @block.sync
            def _(sp):
                sp.dma_start(out.rearrange("b (h p) d -> p (b h) d", p=P), k.X[:, :, :]).then_inc(stored, 16)
                sp.wait_ge(stored, 16)


def host_constants():
    f = np.float32
    lower = np.tril(np.ones((P, P), f))
    inv = (f(1.0) / f(10000.0) ** (np.arange(0, HSA, 2, dtype=f) / f(HSA))).astype(f)
    ang = np.arange(T, dtype=f)[:, None] * inv[None, :]
    c, s = np.cos(ang).astype(f), np.sin(ang).astype(f)
    cos = np.concatenate([c, c], 1).reshape(2, P, HSA)
    sin = np.concatenate([-s, s], 1).reshape(2, P, HSA)
    scale = np.array([HSA ** -0.5, 1.0], f)
    out = {
        "ident": np.eye(P, dtype=f),
        "tri_incl": np.ascontiguousarray(lower.T),
        "tri_strict": np.ascontiguousarray(np.triu(np.ones((P, P), f), 1)),
        "a_cos": np.ascontiguousarray((cos[:, :, None, :] * scale[None, None, :, None]).transpose(1, 0, 2, 3)),
        "a_sin": np.ascontiguousarray((sin[:, :, None, :] * scale[None, None, :, None]).transpose(1, 0, 2, 3)),
        "a_head_rows": np.repeat(np.eye(HPT, dtype=f), HSA, 0),
    }
    out["m_expert_no"] = np.tile(np.arange(E, dtype=f), (P, 1))
    out["zeros"] = np.zeros((P, E * CAP * H // P), f)
    out["after"] = np.ascontiguousarray(np.tril(np.ones((P, P), f), -1))
    i, j = np.arange(P)[:, None], np.arange(P)[None, :]
    out["off_mask"] = np.ascontiguousarray(np.stack(
        [((i // s) % 2 == 1) & (j // s == i // s - 1) for s in LEVELS], 1).astype(f))
    out["pair_mask"] = ((j % 2 == 1) & (i == j - 1)).astype(f)
    return out


def lay_out(x):
    c = np.ascontiguousarray
    g = {n: np.asarray(a) for n, a in x.items()}
    a = "L0_attn_a_"
    even_odd = np.arange(H).reshape(NHA, HSA // 2, 2).transpose(0, 2, 1).ravel()
    w = np.concatenate([g[a + "Wq"][:, even_odd], g[a + "Wk"][:, even_odd], g[a + "Wv"]], 1)
    out = {
        "x": c(g[a + "x"]),
        "a_w_qkv": c(w.reshape(KC, P, 3 * H).transpose(1, 0, 2)),
        "a_b_qkv": c(np.concatenate([g[a + "bq"][even_odd], g[a + "bk"][even_odd], g[a + "bv"]])),
        "a_w_o": c(g[a + "Wo"].reshape(KC, P, H).transpose(1, 0, 2)),
        "a_b_o": c(g[a + "bo"]),
    }
    m = "L0_ffn_"
    gu = np.concatenate([g[m + "w_gate"], g[m + "w_up"]], 2)
    down = np.zeros((len(SHC) * P, H), np.float32)
    down[:IS] = g[m + "ws_down"]
    out.update({
        "m_w_router": c(g[m + "gate_w"].T.reshape(KC, P, E).transpose(1, 0, 2)),
        "m_w_gu": c(gu.reshape(E, KC, P, 2 * I).transpose(0, 2, 1, 3).reshape(E, P, KC * 2 * I)),
        "m_w_d": c(g[m + "w_down"].reshape(E, 2, IH, H).transpose(0, 2, 1, 3).reshape(E, IH, 2 * H)),
        "m_w_sg": c(g[m + "ws_gate"].reshape(KC, P, IS).transpose(1, 0, 2)),
        "m_w_su": c(g[m + "ws_up"].reshape(KC, P, IS).transpose(1, 0, 2)),
        "m_w_sd": c(down.reshape(len(SHC), P, H).transpose(1, 0, 2)),
    })
    d = "L0_attn_b_"
    wt = g[d + "w_qkvz"].reshape(NP, 2, 4, D, KC, P).transpose(0, 5, 4, 2, 1, 3).reshape(NP, P, KC * 4 * P)
    taps = g[d + "conv_w"].reshape(3, NP, P, TAPS).transpose(1, 2, 0, 3).reshape(NP, P, 3 * TAPS)
    ba = g[d + "w_ba"].reshape(NH, 2, KC, P).transpose(3, 2, 1, 0).reshape(P, KC, 2 * NH)
    out.update({
        "d_w_pair": c(np.concatenate([wt, taps], 2)),
        "d_w_ba": c(ba),
        "d_w_out": c(g[d + "w_out"].T.reshape(NP, P, H)),
        "d_a_log": c(g[d + "A_log"]),
        "d_dt_bias": c(g[d + "dt_bias"]),
        "d_norm_w": c(np.concatenate([g[d + "norm_weight"]] * 2)[:, None]),
    })
    return out


def kernel(**inputs):
    import concourse.bacc as _bacc
    from concourse.bass_utils import run_bass_kernel_spmd as _run

    nc = _bacc.Bacc("TRN2", target_bir_lowering=False, num_devices=1)
    arrays = {**host_constants(), **lay_out(inputs)}
    I_ = {n: nc.dram_tensor("in_" + n, a.shape, mybir.dt.from_np(a.dtype), kind="ExternalInput").ap()
          for n, a in arrays.items()}
    out = nc.dram_tensor("out_x", [B, T, H], F32, kind="ExternalOutput").ap()
    build(nc, I_, out)
    r = _run(nc, [{"in_" + n: a for n, a in arrays.items()}], core_ids=[0])
    return r.results[0]["out_x"]
```
